# Optimizing a Trainium2 kernel written in Bass

```python
import numpy as np
import jax
import jax.numpy as jnp

def _softmax(x, axis=-1):
    return jax.nn.softmax(x, axis=axis)

def _gelu(x):
    return jax.nn.gelu(x, approximate=True)

def _silu(x):
    return jax.nn.silu(x)

def _sigmoid(x):
    return jax.nn.sigmoid(x)

def _layernorm(x, axis=-1, eps=1e-05):
    m = jnp.mean(x, axis=axis, keepdims=True)
    v = jnp.var(x, axis=axis, keepdims=True)
    return (x - m) / jnp.sqrt(v + eps)

def _scatter_add(tgt, idx, src, axis=0):
    return tgt.at[idx].add(src)

def _segment_sum(src, seg, n):
    return jax.ops.segment_sum(src, seg, n)
kernel_name = 'mk_seq_postln_d2_jaxref_r8_52eb91'

def setup_inputs(seed: int=0):
    np.random.seed(seed)
    _w = jnp.asarray

    def _L0_attn_setup():
        import jax, jax.numpy as jnp
        import numpy as np
        EPS = 1.1920929e-07

        def _rms(x):
            return x * jax.lax.rsqrt(jnp.mean(x * x, axis=-1, keepdims=True) + EPS)
        key = jax.random.key(seed)
        k0, k1, k2, k3 = jax.random.split(key, 4)
        B, S, D, DFF = (4, 256, 256, 1024)
        x = jax.random.normal(k0, (B, S, D), dtype=jnp.float32)
        w_qkv = jax.random.normal(k1, (3 * D, D), dtype=jnp.float32) * 0.02
        w_swiglu = jax.random.normal(k2, (2 * DFF, D), dtype=jnp.float32) * 0.02
        w_out = jax.random.normal(k3, (D, DFF), dtype=jnp.float32) * 0.02
        return {'x': x, 'w_qkv': w_qkv, 'w_swiglu': w_swiglu, 'w_out': w_out}
    _L0_attn_in = _L0_attn_setup()

    def _L0_ffn_setup():
        import jax, jax.numpy as jnp
        import numpy as np
        B, S, D, E, R, TOP_K = (4, 512, 256, 6, 16, 2)
        key = jax.random.key(seed)
        ks = jax.random.split(key, 9)
        scale = 0.02
        return {'x': jax.random.normal(ks[0], (B, S, D), dtype=jnp.float32), 'W_base': jax.random.normal(ks[1], (D, D), dtype=jnp.float32) * scale, 'b_base': jax.random.normal(ks[2], (D,), dtype=jnp.float32) * scale, 'A_s': jax.random.normal(ks[3], (D, R), dtype=jnp.float32) * scale, 'B_s': jax.random.normal(ks[4], (R, D), dtype=jnp.float32) * scale, 'A_r': jax.random.normal(ks[5], (E, D, R), dtype=jnp.float32) * scale, 'B_r': jax.random.normal(ks[6], (E, R, D), dtype=jnp.float32) * scale, 'W_router': jax.random.normal(ks[7], (D, E), dtype=jnp.float32) * scale, 'b_router': jax.random.normal(ks[8], (E,), dtype=jnp.float32) * scale}
    _L0_ffn_in = _L0_ffn_setup()

    def _L1_attn_setup():
        import jax, jax.numpy as jnp
        import numpy as np
        B_, L_, D_MODEL = (2, 512, 256)
        EXPAND, HEADDIM, DCONV = (2, 64, 4)
        INNER = EXPAND * D_MODEL
        NHEADS = INNER // HEADDIM
        key = jax.random.key(seed)
        ks = jax.random.split(key, 8)
        f32 = jnp.float32
        return {'hidden_states': jax.random.normal(ks[0], (B_, L_, D_MODEL), f32), 'in_proj_w': jax.random.normal(ks[1], (INNER, D_MODEL), f32) * 0.02, 'gate_proj_w': jax.random.normal(ks[2], (INNER, D_MODEL), f32) * 0.02, 'out_proj_w': jax.random.normal(ks[3], (D_MODEL, INNER), f32) * 0.02, 'conv_w': jax.random.normal(ks[4], (INNER, DCONV), f32) * 0.02, 'conv_b': jnp.zeros((INNER,), f32), 'dt_w': jax.random.normal(ks[5], (NHEADS, HEADDIM), f32) * 0.02, 'dt_b': jnp.zeros((NHEADS,), f32), 'A_log': jnp.zeros((NHEADS, HEADDIM), f32), 'Bp': jax.random.normal(ks[6], (NHEADS, HEADDIM), f32) * 0.02, 'Cp': jax.random.normal(ks[7], (NHEADS, HEADDIM), f32) * 0.02, 'Dp': jnp.ones((NHEADS, HEADDIM), f32)}
    _L1_attn_in = _L1_attn_setup()

    def _L1_ffn_setup():
        import jax, jax.numpy as jnp
        import numpy as np
        B, S, H = (2, 128, 256)
        E, K, F = (8, 2, 176)
        N_SHARED = 2
        FS = F * N_SHARED
        ROUTED_SCALE = 1.0

        def _swiglu_mlp(x, wg, wu, wd):
            return jax.nn.silu(x @ wg.T) * (x @ wu.T) @ wd.T
        key = jax.random.key(seed)
        ks = jax.random.split(key, 8)

        def w(k, shape, fan_in):
            return jax.random.normal(k, shape, jnp.float32) * (1.0 / np.sqrt(fan_in))
        return {'hidden_states': jax.random.normal(ks[0], (B, S, H), jnp.float32), 'gate_weight': w(ks[1], (E, H), H), 'w_gate': w(ks[2], (E, F, H), H), 'w_up': w(ks[3], (E, F, H), H), 'w_down': w(ks[4], (E, H, F), F), 'sw_gate': w(ks[5], (FS, H), H), 'sw_up': w(ks[6], (FS, H), H), 'sw_down': w(ks[7], (H, FS), FS)}
    _L1_ffn_in = _L1_ffn_setup()
    _d = {'L0_attn_x': _L0_attn_in['x'], 'L0_attn_w_qkv': _L0_attn_in['w_qkv'], 'L0_attn_w_swiglu': _L0_attn_in['w_swiglu'], 'L0_attn_w_out': _L0_attn_in['w_out'], 'L0_ffn_W_base': _L0_ffn_in['W_base'], 'L0_ffn_b_base': _L0_ffn_in['b_base'], 'L0_ffn_A_s': _L0_ffn_in['A_s'], 'L0_ffn_B_s': _L0_ffn_in['B_s'], 'L0_ffn_A_r': _L0_ffn_in['A_r'], 'L0_ffn_B_r': _L0_ffn_in['B_r'], 'L0_ffn_W_router': _L0_ffn_in['W_router'], 'L0_ffn_b_router': _L0_ffn_in['b_router'], 'L1_attn_in_proj_w': _L1_attn_in['in_proj_w'], 'L1_attn_gate_proj_w': _L1_attn_in['gate_proj_w'], 'L1_attn_out_proj_w': _L1_attn_in['out_proj_w'], 'L1_attn_conv_w': _L1_attn_in['conv_w'], 'L1_attn_conv_b': _L1_attn_in['conv_b'], 'L1_attn_dt_w': _L1_attn_in['dt_w'], 'L1_attn_dt_b': _L1_attn_in['dt_b'], 'L1_attn_A_log': _L1_attn_in['A_log'], 'L1_attn_Bp': _L1_attn_in['Bp'], 'L1_attn_Cp': _L1_attn_in['Cp'], 'L1_attn_Dp': _L1_attn_in['Dp'], 'L1_ffn_gate_weight': _L1_ffn_in['gate_weight'], 'L1_ffn_w_gate': _L1_ffn_in['w_gate'], 'L1_ffn_w_up': _L1_ffn_in['w_up'], 'L1_ffn_w_down': _L1_ffn_in['w_down'], 'L1_ffn_sw_gate': _L1_ffn_in['sw_gate'], 'L1_ffn_sw_up': _L1_ffn_in['sw_up'], 'L1_ffn_sw_down': _L1_ffn_in['sw_down']}
    _x0 = _d['L0_attn_x']
    _d['L0_attn_x'] = jax.random.normal(jax.random.fold_in(jax.random.key(seed), 1), (2, 2048, 256), dtype=_x0.dtype)
    del _x0
    return _d

def reference(L0_attn_x, L0_attn_w_qkv, L0_attn_w_swiglu, L0_attn_w_out, L0_ffn_W_base, L0_ffn_b_base, L0_ffn_A_s, L0_ffn_B_s, L0_ffn_A_r, L0_ffn_B_r, L0_ffn_W_router, L0_ffn_b_router, L1_attn_in_proj_w, L1_attn_gate_proj_w, L1_attn_out_proj_w, L1_attn_conv_w, L1_attn_conv_b, L1_attn_dt_w, L1_attn_dt_b, L1_attn_A_log, L1_attn_Bp, L1_attn_Cp, L1_attn_Dp, L1_ffn_gate_weight, L1_ffn_w_gate, L1_ffn_w_up, L1_ffn_w_down, L1_ffn_sw_gate, L1_ffn_sw_up, L1_ffn_sw_down):

    def _L0_attn_ref(x, w_qkv, w_swiglu, w_out):
        import jax, jax.numpy as jnp
        import numpy as np
        EPS = 1.1920929e-07

        def _rms(x):
            return x * jax.lax.rsqrt(jnp.mean(x * x, axis=-1, keepdims=True) + EPS)
        qkv = _rms(x) @ w_qkv.T
        q, k, v = jnp.split(qkv, 3, axis=-1)
        q = _rms(q)
        k = _rms(k)
        w = jnp.exp(k)
        kv_cum = jnp.cumsum(w * v, axis=1)
        w_cum = jnp.cumsum(w, axis=1)
        y = jax.nn.sigmoid(q) * (kv_cum / (w_cum + 1e-06))
        uv = y @ w_swiglu.T
        u, g = jnp.split(uv, 2, axis=-1)
        return x + u * jax.nn.silu(g) @ w_out.T

    def _L0_ffn_ref(x, W_base, b_base, A_s, B_s, A_r, B_r, W_router, b_router):
        import jax, jax.numpy as jnp
        import numpy as np
        B, S, D, E, R, TOP_K = (4, 512, 256, 6, 16, 2)
        base_out = jax.lax.stop_gradient(jnp.einsum('bsd,df->bsf', x, W_base) + b_base)
        shared_out = jnp.einsum('bsr,rf->bsf', jnp.einsum('bsd,dr->bsr', x, A_s), B_s)
        gates = jax.nn.softmax(jnp.einsum('bsd,de->bse', x, W_router) + b_router, axis=-1)
        topk_w, topk_i = jax.lax.top_k(gates, TOP_K)
        w_per_e = jnp.sum(topk_w[..., None] * jax.nn.one_hot(topk_i, E, dtype=x.dtype), axis=2)
        h = jnp.einsum('bsd,edr->bser', x, A_r)
        hw = h * w_per_e[..., None]
        routed_out = jnp.einsum('bser,erf->bsf', hw, B_r)
        return base_out + shared_out + routed_out

    def _L1_attn_ref(hidden_states, in_proj_w, gate_proj_w, out_proj_w, conv_w, conv_b, dt_w, dt_b, A_log, Bp, Cp, Dp):
        import jax, jax.numpy as jnp
        import numpy as np
        B_, L_, D_MODEL = (2, 512, 256)
        EXPAND, HEADDIM, DCONV = (2, 64, 4)
        INNER = EXPAND * D_MODEL
        NHEADS = INNER // HEADDIM
        B, L, _ = hidden_states.shape
        proj = hidden_states @ in_proj_w.T
        gate = jax.nn.sigmoid(hidden_states @ gate_proj_w.T)
        xp = jnp.pad(proj, ((0, 0), (DCONV - 1, 0), (0, 0)))
        conv = conv_b
        for k in range(DCONV):
            conv = conv + xp[:, k:k + L, :] * conv_w[:, k]
        conv = jax.nn.silu(conv)
        X = conv.reshape(B, L, NHEADS, HEADDIM)
        dt = jnp.einsum('blhp,hp->blh', X, dt_w) + dt_b
        dt = jax.nn.softplus(dt)
        A = -jnp.exp(A_log)
        decay = jnp.exp(dt[..., None] * A)
        drive = dt[..., None] * Bp * X

        def step(s, xs):
            d_t, b_t = xs
            s = d_t * s + b_t
            return (s, s)
        s0 = jnp.zeros((B, NHEADS, HEADDIM), X.dtype)
        _, states = jax.lax.scan(step, s0, (jnp.moveaxis(decay, 1, 0), jnp.moveaxis(drive, 1, 0)))
        states = jnp.moveaxis(states, 0, 1)
        y = Cp * states + Dp * X
        combined = y.reshape(B, L, INNER) * gate
        return combined @ out_proj_w.T

    def _L1_ffn_ref(hidden_states, gate_weight, w_gate, w_up, w_down, sw_gate, sw_up, sw_down):
        import jax, jax.numpy as jnp
        import numpy as np
        B, S, H = (2, 128, 256)
        E, K, F = (8, 2, 176)
        N_SHARED = 2
        FS = F * N_SHARED
        ROUTED_SCALE = 1.0

        def _swiglu_mlp(x, wg, wu, wd):
            return jax.nn.silu(x @ wg.T) * (x @ wu.T) @ wd.T
        b, s, h = hidden_states.shape
        x = hidden_states.reshape(-1, h)
        T = x.shape[0]
        logits = x.astype(jnp.float32) @ gate_weight.astype(jnp.float32).T
        scores = jax.nn.softmax(logits, axis=-1)
        topk_w, topk_idx = jax.lax.top_k(scores, K)
        topk_w = topk_w / (jnp.sum(topk_w, axis=-1, keepdims=True) + 1e-20)
        topk_w = topk_w * ROUTED_SCALE
        cw = jnp.zeros((T, E), jnp.float32).at[jnp.arange(T)[:, None], topk_idx].add(topk_w)
        g = jax.nn.silu(jnp.einsum('th,efh->tef', x, w_gate)) * jnp.einsum('th,efh->tef', x, w_up)
        expert_out = jnp.einsum('tef,ehf->teh', g, w_down)
        y = jnp.einsum('te,teh->th', cw, expert_out).reshape(b, s, h)
        y = y + _swiglu_mlp(x, sw_gate, sw_up, sw_down).reshape(b, s, h)
        return y
    x = L0_attn_x
    x = _layernorm(x + _L0_attn_ref(x, L0_attn_w_qkv, L0_attn_w_swiglu, L0_attn_w_out), axis=-1)
    x = _layernorm(x + _L0_ffn_ref(x, L0_ffn_W_base, L0_ffn_b_base, L0_ffn_A_s, L0_ffn_B_s, L0_ffn_A_r, L0_ffn_B_r, L0_ffn_W_router, L0_ffn_b_router), axis=-1)
    x = _layernorm(x + _L1_attn_ref(x, L1_attn_in_proj_w, L1_attn_gate_proj_w, L1_attn_out_proj_w, L1_attn_conv_w, L1_attn_conv_b, L1_attn_dt_w, L1_attn_dt_b, L1_attn_A_log, L1_attn_Bp, L1_attn_Cp, L1_attn_Dp), axis=-1)
    x = _layernorm(x + _L1_ffn_ref(x, L1_ffn_gate_weight, L1_ffn_w_gate, L1_ffn_w_up, L1_ffn_w_down, L1_ffn_sw_gate, L1_ffn_sw_up, L1_ffn_sw_down), axis=-1)
    return x

_drawn_inputs = setup_inputs


def setup_inputs(seed=0):
    import zlib

    import numpy as np

    out = dict(_drawn_inputs(seed))
    spreads = {'L1_attn_conv_b': (0.0, 0.1),
     'L1_attn_dt_b': (0.0, 2.0),
     'L1_attn_A_log': (0.0, 2.0),
     'L1_attn_Dp': (1.0, 0.6)}
    factors = {'L0_attn_w_qkv': 8.0,
     'L0_attn_w_swiglu': 8.0,
     'L0_attn_w_out': 8.0,
     'L0_ffn_W_router': 9.178,
     'L0_ffn_b_router': 59.392,
     'L1_attn_in_proj_w': 8.0,
     'L1_attn_gate_proj_w': 5.68,
     'L1_attn_conv_w': 6.555,
     'L1_attn_dt_w': 63.551,
     'L1_attn_Bp': 36.898,
     'L1_attn_Cp': 44.48}
    for name, (base, spread) in spreads.items():
        noise = np.random.default_rng([zlib.crc32(name.encode()), seed]).standard_normal(out[name].shape)
        drawn = base * np.exp(spread * noise) if base else spread * noise
        out[name] = jnp.asarray(drawn.astype(out[name].dtype))
    for name, factor in factors.items():
        out[name] = (out[name] * factor).astype(out[name].dtype)
    return out
```

```python
from contextlib import ExitStack

import numpy as np
import concourse.bass as bass
from concourse import mybir

ALU = mybir.AluOpType
ACT = mybir.ActivationFunctionType
F32 = mybir.dt.float32
F16 = mybir.dt.float16
BF16 = mybir.dt.bfloat16
U32 = mybir.dt.uint32
AX_X = mybir.AxisListType.X

P = 128
B, S, D = 2, 2048, 256
N = 512
CH = S // N
TT = N // P
KD = D // P
DFF = 1024
E0, R0 = 6, 16
ER = E0 * R0
HL = ER + R0
INNER, NH, DCONV = 512, 8, 4
CT = INNER // P
E1, F1, FS = 8, 176, 352
HID = E1 * F1 + FS
RT = E1 * F1 // P
EPS_RMS, EPS_LN = 1.1920929e-07, 1e-05
WS = 256.0
IWS = 1.0 / WS
G = 8
NEG = -3.0e38
HT0 = DFF // P
HT1 = -(-HID // P)
NB, NBL = 4, 2
HR = 4

W_PARTS = [("qkv", KD * 3 * D), ("swi", KD * 2 * DFF), ("wo", HT0 * D), ("lora_a", KD * HL), ("route0", KD * E0),
           ("base", KD * D), ("lora_b", D), ("inp", KD * INNER), ("gatep", KD * INNER), ("outp", CT * D),
           ("route1", KD * E1), ("eg", KD * HID), ("eu", KD * HID), ("ed", HT1 * D)]
W_AT = {}
W_COLS = 0
for _n, _c in W_PARTS:
    W_AT[_n] = (W_COLS, _c)
    W_COLS += _c
PIECES = 11
PC = -(-W_COLS // PIECES)
S_PARTS = [("conv_w", CT * DCONV), ("conv_b", CT), ("A_log", CT), ("Bp", CT), ("Cp", CT), ("Dp", CT), ("dt_b", NH),
           ("dt_w", CT * NH), ("b_router", E0)]
S_AT = {}
S_COLS = 0
for _n, _c in S_PARTS:
    S_AT[_n] = (S_COLS, _c)
    S_COLS += _c
C_PARTS = [("ident", P), ("iota", G), ("sel_q", 2 * P), ("sel_g", HL), ("sel_dt", CT * P), ("sel_cw", RT * P)]
C_AT = {}
C_COLS = 0
for _n, _c in C_PARTS:
    C_AT[_n] = (C_COLS, _c)
    C_COLS += _c


def constants():
    c = np.zeros((P, C_COLS), np.float32)
    c[:, :P] = np.eye(P, dtype=np.float32)
    c[:, C_AT["iota"][0]:C_AT["iota"][0] + G] = np.arange(G, dtype=np.float32)

    def put(name, k, width, column_of):
        for m in range(width):
            for part in range(3):
                c[part * G + column_of(m), C_AT[name][0] + k * width + m] = 1.0

    for j in range(2):
        put("sel_q", j, P, lambda m: j)
    put("sel_g", 0, HL, lambda m: min(m // R0, E0))
    for j in range(CT):
        put("sel_dt", j, P, lambda m: 2 * j + m // (INNER // NH))
    for j in range(RT):
        put("sel_cw", j, P, lambda m: (P * j + m) // F1)
    return c


def light1(s):
    return ([("rms", s, 0), ("xn", s, 0), ("double", s, 0), ("T", s, 0)] + [("qkv", s, j) for j in range(6)]
            + [("sumsq", s, 0), ("rqk", s, 0), ("spread", s, 0), ("qkn", s, 0), ("qkn", s, 1),
               ("cum", s, 0), ("cum", s, 1), ("y", s, 0), ("y", s, 1)])


def light2(s, more):
    return ([("ln", s, 0), ("norm", s, 0), ("T", s, 1), ("route", s, 0), ("h112", s, 0), ("soft", s, 0),
             ("spread", s, 1), ("hw", s, 0), ("out", s, 1), ("ln", s, 1), ("norm", s, 1), ("T", s, 2)]
            + [("pj", s, 0)] + [x for j in range(1, CT) for x in (("pj", s, j), ("silu", s, j - 1))]
            + [("silu", s, CT - 1), ("dt", s, 0), ("softplus", s, 0), ("spread", s, 2), ("ct", s, 0)]
            + [x for j in range(1, CT) for x in (("ct", s, j), ("comb", s, j - 1))] + [("comb", s, CT - 1)] + [("load", s, 0)] * more
            + [("out", s, 2), ("ln", s, 2), ("norm", s, 2), ("T", s, 3), ("route", s, 1), ("soft", s, 1),
               ("spread", s, 3)])


def ffn(name, s, tiles):
    return [(name, s, i) for i in range(tiles + 2)]


def end(s):
    return [("ln", s, 3), ("norm", s, 3), ("store", s, 0)]


def merge(runs, *chains):
    out, done = [], [0, 0]
    for k, n in enumerate(runs):
        out += chains[k % 2][done[k % 2]:done[k % 2] + n]
        done[k % 2] += n
    assert done == [len(c) for c in chains], (done, [len(c) for c in chains])
    return out


def round_of(runs, more):
    return merge(runs, ffn("f0", 0, HT0) + light2(0, more) + ffn("f1", 0, HT1) + end(0) + (light1(0) if more else []),
                 light1(1) + ffn("f0", 1, HT0) + light2(1, more) + ffn("f1", 1, HT1) + end(1))


def with_pieces(order, after):
    out = []
    for k, step in enumerate(order):
        out.append(step)
        out += [("piece", 0, j) for j in after if after[j] == k + 1]
    return out


RUNS = {"body": [0, 1, 2, 1, 1, 1, 2, 1, 1, 1, 3, 1, 1, 1, 2, 4, 5, 2, 1, 5, 1, 1, 2, 1, 1, 1, 4, 2, 3, 2, 2, 4, 2,
                 1, 4, 1, 3, 2, 1, 4, 4, 3, 3, 1, 1, 1, 1, 3, 1, 2, 2, 3, 1, 1, 1, 1, 1, 1, 1, 2, 1, 1, 3, 2, 3, 2,
                 1, 1, 1, 1, 3, 1, 1, 1, 2, 1, 1, 1, 2, 1, 3, 3, 2, 1, 1, 1, 2, 4, 1, 2, 2, 1, 1, 8],
        "epi": [0, 1, 3, 1, 3, 1, 1, 1, 3, 2, 1, 2, 1, 1, 2, 1, 1, 1, 2, 4, 1, 3, 3, 1, 2, 3, 4, 1, 1, 1, 2, 2, 1,
                1, 1, 1, 1, 2, 1, 1, 3, 1, 1, 3, 2, 2, 1, 3, 4, 1, 1, 8, 1, 1, 1, 1, 1, 1, 1, 1, 2, 1, 1, 2, 3, 1,
                1, 2, 1, 1, 3, 2, 2, 2, 1, 3, 3, 19]}
SCHEDULE = {"pro": with_pieces([("load", 0, 0), ("load", 1, 0)] + light1(0), {0: 1, 1: 6, 2: 13}),
            "first": with_pieces(round_of(RUNS["body"], True), {3: 1, 4: 2, 5: 5, 6: 8, 7: 11, 8: 13, 9: 19, 10: 23}),
            "body": round_of(RUNS["body"], True), "epi": round_of(RUNS["epi"], False)}
REGIONS = ("pro", "first", "body", "epi")


def tiles_of(name, i):
    if name == "T":
        return [(k, "light") for k in range(KD)]
    if name in ("qkv", "sumsq", "spread", "qkn", "route", "h112", "hw", "pj", "dt"):
        return [(0, "light")]
    if name == "ct":
        return [("dtx", "light"), ("gate", "light")]
    if name == "out":
        return [(0, "light"), (1, "light")]
    if name in ("f0", "f1"):
        t = [(0, 0), (1, 1)] if i == 2 else []
        n = HT0 if name == "f0" else HT1
        if i < n:
            t += [("g", "hidden"), ("u", "hidden")]
            if name == "f1" and i < RT:
                t.append(("cw", "hidden"))
        return t
    return []


class Banks:

    def __init__(self):
        self.place, self.totals, self.base, self.last = {}, {}, {}, {}
        before = {b: 0 for b in range(8)}
        for region in REGIONS:
            used = {b: 0 for b in range(8)}
            last = {}
            ring = {"hidden": 0, "light": 0}
            for name, s, i in SCHEDULE[region]:
                for tile, where in tiles_of(name, i):
                    if where == "hidden":
                        b = 2 + ring[where] % NB
                    elif where == "light":
                        b = 2 + NB + ring[where] % NBL
                    else:
                        b = where
                    if where in ring:
                        ring[where] += 1
                    self.place[region, name, s, i, tile] = (b, used[b], last.get(b))
                    last[b] = (name, s, i, tile)
                    used[b] += 1
            self.totals[region], self.base[region], self.last[region] = used, dict(before), last
            times = CH - 2 if region == "body" else 1
            before = {b: before[b] + times * used[b] for b in range(8)}


def hidden_index():
    first, n = {}, {}
    for region in SCHEDULE:
        n[region] = 0
        for name, s, i in SCHEDULE[region]:
            if name in ("f0", "f1") and i == 0:
                first[region, name, s] = n[region]
                n[region] += HT0 if name == "f0" else HT1
    return first, n["body"]


class Signal:

    def __init__(self, sem, name, per):
        self.name, self.per = name, per
        self.sems = [sem(f"{name}{s}") for s in range(B)]
        self.n = [0] * B

    def __getitem__(self, s):
        return self.sems[s]

    def at(self, c, j):
        it, ahead = c
        return it * self.per + (ahead * self.per + j)

    def start(self, s):
        assert self.n[s] in (0, self.per), (self.name, self.n)
        self.n[s] = 0

    def one(self, s):
        self.n[s] += 1
        return 1

    def last(self, s, c):
        return self.at(c, self.n[s])


def bass_two_postnorm_layers(nc, x, wpack, small, const, out):
    banks = Banks()
    hidden_first, HB = hidden_index()
    assert HB % HR == 0

    with ExitStack() as ctx:
        def sb(name, shape, dt=F32):
            return ctx.enter_context(nc.sbuf_tensor(name, shape, dt))

        def sem(name):
            return ctx.enter_context(nc.semaphore(name))

        def sems(name):
            return [sem(f"{name}{s}") for s in range(B)]

        bank = [ctx.enter_context(nc.psum_tensor(f"bank{b}", [P, N], F32)) for b in range(8)]

        Wh, Wl = sb("Wh", [P, W_COLS], F16), sb("Wl", [P, W_COLS], F16)
        sm = sb("sm", [P, S_COLS])
        ident = sb("ident", [P, P])
        identb = sb("identb", [P, P], BF16)
        iota = sb("iota", [P, G])
        sel = sb("sel", [P, C_COLS - P - G], BF16)
        zero = sb("zero", [P, 1])
        ones = sb("ones", [P, 1])
        eps = sb("eps", [P, 2, TT])
        idle = sb("idle", [P, 2 * B])
        neghalf = sb("neghalf", [P, TT * G])
        BC = sb("BC", [P, CT])
        Dh = sb("Dh", [P, CT])
        negA = sb("negA", [P, CT])
        tok = [sb(f"tok{s}", [P, TT, D]) for s in range(B)]
        xTh = [sb(f"xTh{s}", [P, KD, N], F16) for s in range(B)]
        xTl = [sb(f"xTl{s}", [P, KD, N], F16) for s in range(B)]
        slot = [sb(f"slot{s}", [P, 10, N]) for s in range(B)]
        xin = [slot[s][:, 8:10, :].rearrange("p a (t d) -> p (a t) d", d=D) for s in range(B)]
        cTh = [sb(f"cTh{s}", [P, CT, N], F16) for s in range(B)]
        cTl = [sb(f"cTl{s}", [P, CT, N], F16) for s in range(B)]
        hwh, hwl = sb("hwh", [P, N], F16), sb("hwl", [P, N], F16)
        HIST = DCONV - 1
        pj = [sb(f"pj{s}", [P, CT, HIST + N]) for s in range(B)]
        partsT = [sb(f"partsT{s}", [3 * G, N], BF16) for s in range(B)]
        small8 = [sb(f"small8{s}", [P, TT, G]) for s in range(B)]
        rest = [sb(f"rest{s}", [P, TT, G]) for s in range(B)]
        parts = [sb(f"parts{s}", [P, TT, 3, G], BF16) for s in range(B)]
        logit = [sb(f"logit{s}", [P, 2, TT, G]) for s in range(B)]
        top8 = [sb(f"top8{s}", [P, TT, G]) for s in range(B)]
        idx8 = [sb(f"idx8{s}", [P, TT, G], U32) for s in range(B)]
        mask = [sb(f"mask{s}", [P, 2, TT, G]) for s in range(B)]
        prob = [sb(f"prob{s}", [P, TT, G]) for s in range(B)]
        dtb = [sb(f"dtb{s}", [P, 2, TT, G]) for s in range(B)]
        stat = [sb(f"stat{s}", [P, 3, TT]) for s in range(B)]
        bn = [sb(f"bn{s}", [P, TT, 6]) for s in range(B)]
        mv = [sb(f"mv{s}", [P, TT, 2]) for s in range(B)]
        carry0 = [sb(f"carry0{s}", [P, 2 * KD]) for s in range(B)]
        carry1 = [sb(f"carry1{s}", [P, CT]) for s in range(B)]
        sg = sb("sg", [P, 2, N])
        h32 = sb("h32", [P, 2, N])
        hTh = sb("hTh", [P, HR, N], F16)
        hTl = sb("hTl", [P, HR, N], F16)

        sm_stat = [sb(f"sm_stat{s}", [P, 3, TT]) for s in range(B)]

        full = [sem(f"bank_full{b}") for b in range(8)]
        piece_in = [sem(f"piece_in{j}") for j in range(2)]
        consts_in, consts_ok = sem("consts_in"), sem("consts_ok")
        piece_hi, piece_lo = sem("piece_hi"), sem("piece_lo")
        prep_a, prep_p, prep_v = sem("prep_a"), sem("prep_p"), sem("prep_v")
        silu_ok, h_ok = sem("silu_ok"), sem("h_ok")
        h_hi, h_lo, down_ok = sem("h_hi"), sem("h_lo"), sem("down_ok")

        x_in, stored = Signal(sem, "x_in", 16), Signal(sem, "stored", 16)
        squares = Signal(sem, "squares", 1)
        rstd = Signal(sem, "rstd", 5)
        var = Signal(sem, "var", 4)
        normed = Signal(sem, "normed", 5)
        x2 = Signal(sem, "x2", 1)
        xT_hi, xT_lo = Signal(sem, "xT_hi", 8), Signal(sem, "xT_lo", 8)
        qkv_in = Signal(sem, "qkv_in", 6)
        sq_in = Signal(sem, "sq_in", 4)
        ms_qk, rqk_ok = Signal(sem, "ms_qk", 1), Signal(sem, "rqk_ok", 1)
        parts_ok = Signal(sem, "parts_ok", 4)
        partsT_ok = Signal(sem, "partsT_ok", 4)
        qk_normed = Signal(sem, "qk_normed", 4)
        qk_exp = Signal(sem, "qk_exp", 4)
        den_ok, y_ok = Signal(sem, "den_ok", 2), Signal(sem, "y_ok", 2)
        c_hi, c_lo = Signal(sem, "c_hi", 6), Signal(sem, "c_lo", 6)
        logits = Signal(sem, "logits", 2)
        soft_in, soft_exp = Signal(sem, "soft_in", 2), Signal(sem, "soft_exp", 2)
        h_in, hw_ok = Signal(sem, "h_in", 1), Signal(sem, "hw_ok", 1)
        hw_hi, hw_lo = Signal(sem, "hw_hi", 1), Signal(sem, "hw_lo", 1)
        pj_in, tap0 = Signal(sem, "pj_in", 4), Signal(sem, "tap0", 4)
        conv_ok, X_ok = Signal(sem, "conv_ok", 4), Signal(sem, "X_ok", 4)
        dt_abs, dt_exp, dt_ln = Signal(sem, "dt_abs", 1), Signal(sem, "dt_exp", 1), Signal(sem, "dt_ln", 1)
        decay_ok, drive_ok = Signal(sem, "decay_ok", 4), Signal(sem, "drive_ok", 4)
        tanh_ok, comb_ok = Signal(sem, "tanh_ok", 4), Signal(sem, "comb_ok", 4)
        own_v = Signal(sem, "own_v", 86)
        own_p = Signal(sem, "own_p", 5)
        hist_ok = [sem(f"hist_ok{s}") for s in range(B)]

        def wcols(part, k, width, a=0, n=None):
            at = W_AT[part][0] + k * width + a
            n = width if n is None else n
            return Wh[:, at:at + n], Wl[:, at:at + n]

        def pieces_to(part):
            at, n = W_AT[part]
            return -(-(at + n) // PC)

        def selcols(part, k, width):
            at = C_AT[part][0] - P - G + k * width
            return sel[0:3 * G, at:at + width]

        def smc(part, a=0, n=None):
            at, w = S_AT[part]
            return sm[:, at + a:at + a + (w - a if n is None else n)]

        LIGHT1 = {"rms", "xn", "double", "qkv", "sumsq", "rqk", "qkn", "cum", "y"}

        def chunk(region, it, name, s, i):
            ahead = name == "load" or (s == 0 and (name in LIGHT1 or (name in ("T", "spread") and i == 0)))
            return (0, 0) if region == "pro" else (it, int(ahead))

        class Place:

            def __init__(self, region, it, name, s, i):
                self.region, self.it, self.name, self.s, self.i = region, it, name, s, i
                self.c = chunk(region, it, name, s, i)

            def bank(self, tile=0):
                return banks.place[self.region, self.name, self.s, self.i, tile][0]

            def filled(self, tile=0):
                b, n, _ = banks.place[self.region, self.name, self.s, self.i, tile]
                n += banks.base[self.region][b] + 1
                if self.region == "body":
                    per = banks.totals["body"][b]
                    return self.it * per + (n - per)
                return n

            def number(self, i, name=None):
                return hidden_first[self.region, name or self.name, self.s] + i

            def tile(self, i, back=0, name=None):
                n = self.number(i, name) - back + 1
                return self.it * HB + (max(n, 0) if self.region == "first" else n) + 1

            def used(self, tile=0):
                b, _, last = banks.place[self.region, self.name, self.s, self.i, tile]
                if last is not None:
                    return readers(self.region, self.it, last)
                before = {"pro": None, "first": "pro", "body": "body", "epi": "body"}[self.region]
                if before is None or b not in banks.last[before]:
                    return []
                return readers(before, self.it, banks.last[before][b], 1)

        def readers(region, it, tile, back=0):
            name, s, i, which = tile
            if which in ("g", "u", "cw"):
                n = hidden_first[region, name, s] + i + 2 - back * HB
                return [(silu_ok if which == "g" else h_ok, it * HB + n)]
            it, ahead = chunk(region, it, name, s, i)
            c = (it, ahead - back) if region != "pro" else (0, 0)
            if name == "T":
                found = [(xT_hi, 2 * i + which + 1), (xT_lo, 2 * i + which + 1)]
            elif name == "ct":
                found = [(decay_ok, i + 1), (drive_ok, i + 1)] if which == "dtx" else [(tanh_ok, i + 1)]
            elif name in ("f0", "f1"):
                found = [(var, 1 if name == "f0" else 4)]
            else:
                found = [{"qkv": (qkv_in, i + 1), "sumsq": (ms_qk, 1), "spread": (partsT_ok, i + 1),
                          "qkn": (qk_normed, 2 * i + 2), "route": (logits, i + 1), "h112": (h_in, 1),
                          "hw": (hw_ok, 1), "out": (var, i + 1), "pj": (pj_in, i + 1), "dt": (dt_abs, 1)}[name]]
            return [(signal[s], signal.at(c, j)) for signal, j in found]

        def walk(engine, steps):
            for region in REGIONS:
                if region == "body":
                    with engine.Fori(1, CH - 1) as it:
                        for name, s, i in SCHEDULE[region]:
                            if name in steps:
                                steps[name](Place(region, it, name, s, i), s, i)
                else:
                    for name, s, i in SCHEDULE[region]:
                        if name in steps:
                            steps[name](Place(region, CH - 1 if region == "epi" else 0, name, s, i), s, i)

        block = ctx.enter_context(nc.Block())

        @block.sync
        def _(sp):
            def load(at, s, i):
                if at.region != "pro":
                    sp.wait_ge(comb_ok[s], comb_ok.at((at.it, 0), CT))
                src = x[s][bass.ds((at.c[0] + at.c[1]) * N, N), :].rearrange("(t p) d -> p t d", p=P)
                sp.dma_start(xin[s], src).then_inc(x_in[s], 16)

            def store(at, s, i):
                sp.wait_ge(normed[s], normed.at(at.c, 5))
                dst = out[s][bass.ds((at.c[0] + at.c[1]) * N, N), :].rearrange("(t p) d -> p t d", p=P)
                sp.dma_start(dst, tok[s][:]).then_inc(stored[s], 16)

            def piece(at, s, j):
                if j >= 2:
                    sp.wait_ge(piece_hi, j - 1)
                    sp.wait_ge(piece_lo, j - 1)
                a, n = j * PC, min(PC, W_COLS - j * PC)
                stage = pj[j % 2][:].rearrange("p a n -> p (a n)")
                sp.dma_start(stage[:, 0:n], wpack[:, a:a + n]).then_inc(piece_in[j % 2], 16)

            sp.dma_start(sm[:], small).then_inc(consts_in, 16)
            stage = slot[1][:, 0:5, :].rearrange("p a n -> p (a n)")
            sp.dma_start(stage[:, 0:C_COLS], const).then_inc(consts_in, 16)
            walk(sp, {"load": load, "store": store, "piece": piece})
            for s in range(B):
                sp.wait_ge(stored[s], stored.at((CH, 0), 0))

        @block.tensor
        def _(pe):
            def mm3(dst, lhs, rhs, first, last):
                pe.matmul(dst, lhs[0], rhs[0], start=first, stop=False, skip_group_check=True)
                pe.matmul(dst, lhs[0], rhs[1], start=False, stop=False, skip_group_check=True)
                return pe.matmul(dst, lhs[1], rhs[0], start=False, stop=last, skip_group_check=True)

            def weights(at, part):
                if at.region in ("pro", "first"):
                    pe.wait_ge(piece_hi, pieces_to(part))
                    pe.wait_ge(piece_lo, pieces_to(part))

            def xT(s, k, t=None):
                c = slice(0, N) if t is None else slice(t * P, (t + 1) * P)
                return xTh[s][:, k, c], xTl[s][:, k, c]

            def T(at, s, t):
                pe.wait_ge(normed[s], normed.at(at.c, t + 1))
                if at.region == "pro":
                    pe.wait_ge(consts_ok, 1)
                src = slot[s][:, 0:2, :].rearrange("p a (t d) -> p (a t) d", d=D) if t == 0 else tok[s]
                for k in range(KD):
                    for reader, n in at.used(k):
                        pe.wait_ge(reader, n)
                    b = at.bank(k)
                    for tt in range(TT):
                        mm = pe.transpose(bank[b][:, tt * P:(tt + 1) * P], src[:, tt, k * P:(k + 1) * P], ident[:])
                    mm.then_inc(full[b], 1)

            def project(at, tile, part, width, a, m, s):
                for reader, n in at.used(tile):
                    pe.wait_ge(reader, n)
                b = at.bank(tile)
                for k in range(KD):
                    mm = mm3(bank[b][0:m, :], wcols(part, k, width, a, m), xT(s, k), k == 0, k == KD - 1)
                mm.then_inc(full[b], 1)

            def qkv(at, s, j):
                if j == 0:
                    pe.wait_ge(xT_hi[s], xT_hi.at(at.c, 2))
                    pe.wait_ge(xT_lo[s], xT_lo.at(at.c, 2))
                    weights(at, "qkv")
                project(at, 0, "qkv", 3 * D, j * P, P, s)

            def sumsq(at, s, i):
                for reader, n in at.used():
                    pe.wait_ge(reader, n)
                b = at.bank()
                for j in range(2):
                    pe.wait_ge(sq_in[s], sq_in.at(at.c, 2 * j + 2))
                    for t in range(TT):
                        for k in range(KD):
                            sq = slot[s][:, 6 + 2 * j + k, t * P:(t + 1) * P]
                            mm = pe.matmul(bank[b][:, t * G + j:t * G + j + 1], sq, ones[:], start=(k == 0),
                                           stop=(k == KD - 1))
                mm.then_inc(full[b], 1)

            def spread(at, s, e):
                for reader, n in at.used():
                    pe.wait_ge(reader, n)
                b = at.bank()
                pe.wait_ge(parts_ok[s], parts_ok.at(at.c, e + 1))
                dst = bank[b][:].bitcast(BF16)
                for t in range(TT):
                    src = parts[s][:, t, :, :].rearrange("p a g -> p (a g)")
                    mm = pe.transpose(dst[0:3 * G, t * P:(t + 1) * P], src, identb[:])
                mm.then_inc(full[b], 1)

            def select(at, tile, part, k, width, s, e):
                for reader, n in at.used(tile):
                    pe.wait_ge(reader, n)
                b = at.bank(tile)
                pe.wait_ge(partsT_ok[s], partsT_ok.at(at.c, e + 1))
                pe.matmul(bank[b][0:width, :], selcols(part, k, width), partsT[s][:], start=True,
                          stop=True).then_inc(full[b], 1)

            def qkn(at, s, j):
                select(at, 0, "sel_q", j, P, s, 0)

            def swiglu(at, s, i):
                one = at.name == "f1"
                tiles = HT1 if one else HT0
                if i == 0 and one:
                    pe.wait_ge(xT_hi[s], xT_hi.at(at.c, 8))
                    pe.wait_ge(xT_lo[s], xT_lo.at(at.c, 8))
                if i == 0 and not one:
                    pe.wait_ge(c_hi[s], c_hi.at(at.c, 2))
                    pe.wait_ge(c_lo[s], c_lo.at(at.c, 2))
                if i == 0:
                    weights(at, "ed" if one else "swi")
                if i < tiles:
                    m = min(P, HID - i * P) if one else P
                    for tile in ("g", "u"):
                        for reader, n in at.used(tile):
                            pe.wait_ge(reader, n)
                        b = at.bank(tile)
                        for k in range(KD):
                            if one:
                                w, rhs = wcols("e" + tile, k, HID, i * P, m), xT(s, k)
                            else:
                                w = wcols("swi", k, 2 * DFF, (DFF if tile == "g" else 0) + i * P, m)
                                rhs = cTh[s][:, k, :], cTl[s][:, k, :]
                            mm = mm3(bank[b][0:m, :], w, rhs, k == 0, k == KD - 1)
                        mm.then_inc(full[b], 1)
                    if one and i < RT:
                        select(at, "cw", "sel_cw", i, P, s, 3)
                j = i - 2
                if j < 0:
                    return
                m = min(P, HID - j * P) if one else P
                if j == 0:
                    for reader, n in at.used(0):
                        pe.wait_ge(reader, n)
                    for reader, n in at.used(1):
                        pe.wait_ge(reader, n)
                    if not one:
                        weights(at, "wo")
                pe.wait_ge(h_hi, at.tile(j))
                pe.wait_ge(h_lo, at.tile(j))
                r = (at.number(j)) % HR
                wh, wl = wcols("ed" if one else "wo", j, D)
                for t in range(TT):
                    c = slice(t * P, (t + 1) * P)
                    mm = mm3(bank[t // 2][:, (t % 2) * D:(t % 2 + 1) * D], (hTh[0:m, r, c], hTl[0:m, r, c]),
                             (wh[0:m], wl[0:m]), j == 0 and t % 2 == 0, j == tiles - 1)
                mm.then_inc(down_ok, 1)

            def route(at, s, m):
                pe.wait_ge(xT_hi[s], xT_hi.at(at.c, 2 * (1 if m == 0 else 3) + 2))
                pe.wait_ge(xT_lo[s], xT_lo.at(at.c, 2 * (1 if m == 0 else 3) + 2))
                part, e = ("route0", E0) if m == 0 else ("route1", E1)
                weights(at, part)
                for reader, n in at.used():
                    pe.wait_ge(reader, n)
                b = at.bank()
                for t in range(TT):
                    for k in range(KD):
                        mm = mm3(bank[b][:, t * G:t * G + e], xT(s, k, t), wcols(part, k, e), k == 0, k == KD - 1)
                mm.then_inc(full[b], 1)

            def h112(at, s, i):
                project(at, 0, "lora_a", HL, 0, HL, s)

            def hw(at, s, i):
                select(at, 0, "sel_g", 0, HL, s, 1)

            def outp(at, s, m):
                weights(at, "lora_b" if m == 1 else "outp")
                for h in range(2):
                    for reader, n in at.used(h):
                        pe.wait_ge(reader, n)
                    b = at.bank(h)
                    if m == 1:
                        pe.wait_ge(hw_hi[s], hw_hi.at(at.c, 1))
                        pe.wait_ge(hw_lo[s], hw_lo.at(at.c, 1))
                    else:
                        pe.wait_ge(c_hi[s], c_hi.at(at.c, 6))
                        pe.wait_ge(c_lo[s], c_lo.at(at.c, 6))
                    for t in range(2 * h, 2 * h + 2):
                        dst = bank[b][:, (t % 2) * D:(t % 2 + 1) * D]
                        c = slice(t * P, (t + 1) * P)
                        if m == 1:
                            for k in range(KD):
                                mm3(dst, xT(s, k, t), wcols("base", k, D), k == 0, False)
                            wh, wl = wcols("lora_b", 0, D)
                            mm = mm3(dst, (hwh[0:HL + 1, c], hwl[0:HL + 1, c]), (wh[0:HL + 1], wl[0:HL + 1]),
                                     False, True)
                        else:
                            for k in range(CT):
                                mm = mm3(dst, (cTh[s][:, k, c], cTl[s][:, k, c]), wcols("outp", k, D), k == 0,
                                         k == CT - 1)
                    mm.then_inc(full[b], 1)

            def pjs(at, s, j):
                if j == 0:
                    pe.wait_ge(xT_hi[s], xT_hi.at(at.c, 6))
                    pe.wait_ge(xT_lo[s], xT_lo.at(at.c, 6))
                    weights(at, "inp")
                project(at, 0, "inp", INNER, j * P, P, s)

            def dts(at, s, i):
                for reader, n in at.used():
                    pe.wait_ge(reader, n)
                b = at.bank()
                pe.wait_ge(X_ok[s], X_ok.at(at.c, 4))
                for t in range(TT):
                    for k in range(CT):
                        mm = pe.matmul(bank[b][:, t * G:t * G + NH], slot[s][:, k, t * P:(t + 1) * P],
                                       smc("dt_w", k * NH, NH), start=(k == 0), stop=(k == CT - 1))
                mm.then_inc(full[b], 1)

            def ct(at, s, j):
                select(at, "dtx", "sel_dt", j, P, s, 2)
                weights(at, "gatep")
                project(at, "gate", "gatep", INNER, j * P, P, s)

            pe.sem_inc(down_ok, 1)
            walk(pe, {"T": T, "qkv": qkv, "sumsq": sumsq, "spread": spread, "qkn": qkn, "f0": swiglu, "f1": swiglu,
                      "route": route, "h112": h112, "hw": hw, "out": outp, "pj": pjs, "dt": dts, "ct": ct})

        @block.scalar
        def _(act):
            def piece(at, s, j):
                a, n = j * PC, min(PC, W_COLS - j * PC)
                act.wait_ge(piece_in[j % 2], 16 * (j // 2 + 1))
                stage = pj[j % 2][:].rearrange("p a n -> p (a n)")
                act.activation(Wh[:, a:a + n], stage[:, 0:n], ACT.Copy, scale=WS).then_inc(piece_hi, 1)

            def rms(at, s, i):
                act.wait_ge(x_in[s], x_in.at(at.c, 16))
                for t in range(TT):
                    ins = act.activation(slot[s][:, 2 + t, 0:D], xin[s][:, t, :], ACT.Square, scale=D ** -0.5,
                                         accum_out=stat[s][:, 0, t:t + 1])
                ins.then_inc(squares[s], 1)

            def T(at, s, t):
                for k in range(KD):
                    act.wait_ge(full[at.bank(k)], at.filled(k))
                    act.activation(xTh[s][:, k, :], bank[at.bank(k)][:], ACT.Copy).then_inc(xT_hi[s], 1)

            def qkv(at, s, j):
                act.wait_ge(full[at.bank()], at.filled())
                act.activation(slot[s][:, j, :], bank[at.bank()][:], ACT.Copy, scale=IWS).then_inc(qkv_in[s], 1)
                if j < 2 * KD:
                    if j == KD:
                        act.wait_ge(x2[s], x2.at(at.c, 1))
                    act.wait_ge(qkv_in[s], qkv_in.at(at.c, j + 1))
                    act.activation(slot[s][:, 6 + j, :], slot[s][:, j, :], ACT.Square).then_inc(sq_in[s], 1)

            def spread(at, s, e):
                act.wait_ge(full[at.bank()], at.filled())
                src = bank[at.bank()][:].bitcast(BF16)[0:3 * G, 0:N]
                act.activation(partsT[s][:], src, ACT.Copy).then_inc(partsT_ok[s], 1)

            def qkn(at, s, j):
                for a in range(2 * j, 2 * j + 2):
                    act.wait_ge(qk_normed[s], qk_normed.at(at.c, a + 1))
                    v = slot[s][:, a, :]
                    act.activation(v, v, ACT.Exp, scale=1.0 if j == 0 else -1.0).then_inc(qk_exp[s], 1)

            def y(at, s, j):
                act.wait_ge(y_ok[s], y_ok.at(at.c, j + 1))
                act.activation(cTh[s][:, j, :], slot[s][:, 2 + j, :], ACT.Copy).then_inc(c_hi[s], 1)

            def swiglu(at, s, i):
                tiles = HT1 if at.name == "f1" else HT0
                if i < tiles:
                    m = min(P, HID - i * P) if at.name == "f1" else P
                    act.wait_ge(full[at.bank("g")], at.filled("g"))
                    g = bank[at.bank("g")]
                    act.wait_ge(h_ok, at.tile(i, 2))
                    r = (at.number(i)) % 2
                    act.activation(sg[0:m, r, :], g[0:m, :], ACT.Silu, scale=IWS).then_inc(silu_ok, 1)
                j = i - 1
                if 0 <= j < tiles:
                    m = min(P, HID - j * P) if at.name == "f1" else P
                    act.wait_ge(h_ok, at.tile(j))
                    act.wait_ge(down_ok, at.tile(j, HR))
                    n = at.number(j)
                    act.activation(hTh[0:m, n % HR, :], h32[0:m, n % 2, :], ACT.Copy).then_inc(h_hi, 1)

            def route(at, s, m):
                act.wait_ge(soft_in[s], soft_in.at(at.c, m + 1))
                act.activation(prob[s][:], prob[s][:], ACT.Exp).then_inc(soft_exp[s], 1)

            def h112(at, s, i):
                act.wait_ge(full[at.bank()], at.filled())
                act.activation(slot[s][0:HL, 0, :], bank[at.bank()][0:HL, :], ACT.Copy,
                               scale=IWS).then_inc(h_in[s], 1)

            def hw(at, s, i):
                act.wait_ge(hw_ok[s], hw_ok.at(at.c, 1))
                act.activation(hwh[0:HL, :], slot[s][0:HL, 0, :], ACT.Copy).then_inc(hw_hi[s], 1)

            def pjs(at, s, j):
                act.wait_ge(hist_ok[s], at.it + 1)
                act.wait_ge(full[at.bank()], at.filled())
                act.activation(pj[s][:, j, HIST:], bank[at.bank()][:], ACT.Copy, scale=IWS).then_inc(pj_in[s], 1)
                act.wait_ge(pj_in[s], pj_in.at(at.c, j + 1))
                act.activation(slot[s][:, j, :], pj[s][:, j, 0:N], ACT.Identity, bias=smc("conv_b", j, 1),
                               scale=smc("conv_w", j * DCONV, 1)).then_inc(tap0[s], 1)

            def silu(at, s, j):
                act.wait_ge(conv_ok[s], conv_ok.at(at.c, j + 1))
                v = slot[s][:, j, :]
                act.activation(v, v, ACT.Silu).then_inc(X_ok[s], 1)

            def softplus(at, s, i):
                act.wait_ge(dt_abs[s], dt_abs.at(at.c, 1))
                v = dtb[s][:, 1, :, :]
                act.activation(v, v, ACT.Exp).then_inc(dt_exp[s], 1)
                act.wait_ge(dt_exp[s], dt_exp.at(at.c, 1))
                act.activation(v, v, ACT.Ln, bias=1.0).then_inc(dt_ln[s], 1)

            def ct(at, s, j):
                if j >= 2:
                    act.wait_ge(comb_ok[s], comb_ok.at(at.c, j - 1))
                act.wait_ge(full[at.bank("dtx")], at.filled("dtx"))
                act.activation(slot[s][:, 4 + j % 2, :], bank[at.bank("dtx")][:], ACT.Exp,
                               scale=negA[:, j:j + 1]).then_inc(decay_ok[s], 1)
                act.wait_ge(full[at.bank("gate")], at.filled("gate"))
                act.activation(slot[s][:, 8 + j % 2, :], bank[at.bank("gate")][:], ACT.Tanh,
                               scale=0.5 * IWS).then_inc(tanh_ok[s], 1)

            def comb(at, s, j):
                act.wait_ge(comb_ok[s], comb_ok.at(at.c, j + 1))
                act.activation(cTh[s][:, j, :], slot[s][:, j, :], ACT.Copy).then_inc(c_hi[s], 1)

            act.sem_inc(silu_ok, 1)
            act.sem_inc(h_hi, 1)
            act.wait_ge(consts_in, 32)
            act.activation(negA[:], smc("A_log"), ACT.Exp).then_inc(prep_a, 1)
            act.wait_ge(consts_ok, 1)
            walk(act, dict(piece=piece, rms=rms, T=T, qkv=qkv, spread=spread, qkn=qkn, y=y, f0=swiglu, f1=swiglu,
                           route=route, h112=h112, hw=hw, pj=pjs, silu=silu, softplus=softplus, ct=ct, comb=comb))

        @block.vector
        def _(dve):
            def pause(s):
                dve.memset(idle[:, s:s + 1], 0.0)

            def piece(at, s, j):
                a, n = j * PC, min(PC, W_COLS - j * PC)
                dve.wait_ge(piece_in[j % 2], 16 * (j // 2 + 1))
                dve.wait_ge(piece_hi, j + 1)
                stage = pj[j % 2][:].rearrange("p a n -> p (a n)")
                dve.scalar_tensor_tensor(out=Wl[:, a:a + n], in0=stage[:, 0:n], scalar=WS, in1=Wh[:, a:a + n],
                                         op0=ALU.mult, op1=ALU.subtract).then_inc(piece_lo, 1)
                if j == PIECES - 1:
                    dve.wait_ge(piece_lo, PIECES)
                    for s in range(B):
                        dve.memset(pj[s][:, :, 0:HIST], 0.0).then_inc(hist_ok[s], 1)

            def xn(at, s, i):
                own_v.start(s)
                dve.wait_ge(x_in[s], x_in.at(at.c, 16))
                dve.wait_ge(rstd[s], rstd.at(at.c, 1))
                dst = slot[s][:, 0:2, :].rearrange("p a (t d) -> p (a t) d", d=D)
                for t in range(TT):
                    ins = dve.tensor_scalar(dst[:, t, :], xin[s][:, t, :], stat[s][:, 2, t:t + 1], None, ALU.mult)
                ins.then_inc(normed[s], 1)

            def T(at, s, t):
                for k in range(KD):
                    dve.wait_ge(full[at.bank(k)], at.filled(k))
                    src = bank[at.bank(k)]
                    dve.wait_ge(xT_hi[s], xT_hi.at(at.c, 2 * t + k + 1))
                    dve.tensor_tensor(xTl[s][:, k, :], src[:], xTh[s][:, k, :],
                                      ALU.subtract).then_inc(xT_lo[s], 1)

            def sumsq(at, s, i):
                dve.wait_ge(full[at.bank()], at.filled())
                src = bank[at.bank()][:, 0:TT * G].rearrange("p (t g) -> p t g", g=G)
                dve.tensor_scalar(rest[s][:, :, 0:2], src[:, :, 0:2], 1.0 / D, EPS_RMS, ALU.mult,
                                  ALU.add).then_inc(ms_qk[s], 1)

            def spread(at, s, e):
                if e == 0:
                    dve.wait_ge(rqk_ok[s], rqk_ok.at(at.c, 1))
                dve.wait_ge(partsT_ok[s], partsT_ok.at(at.c, e))
                p = parts[s]
                dve.tensor_copy(p[:, :, 0, :], small8[s][:]).then_inc(own_v[s], own_v.one(s))
                dve.wait_ge(own_v[s], own_v.last(s, at.c))
                dve.tensor_tensor(rest[s][:], small8[s][:], p[:, :, 0, :], ALU.subtract).then_inc(own_v[s], own_v.one(s))
                dve.wait_ge(own_v[s], own_v.last(s, at.c))
                dve.tensor_copy(p[:, :, 1, :], rest[s][:]).then_inc(own_v[s], own_v.one(s))
                dve.wait_ge(own_v[s], own_v.last(s, at.c))
                dve.tensor_tensor(p[:, :, 2, :], rest[s][:], p[:, :, 1, :],
                                  ALU.subtract).then_inc(parts_ok[s], 1)

            def qkn(at, s, j):
                dve.wait_ge(full[at.bank()], at.filled())
                src = bank[at.bank()]
                for a in range(2 * j, 2 * j + 2):
                    dve.wait_ge(qkv_in[s], qkv_in.at(at.c, a + 1))
                    v = slot[s][:, a, :]
                    dve.tensor_tensor(v, v, src[:], ALU.mult).then_inc(qk_normed[s], 1)

            def cum(at, s, j):
                dve.wait_ge(qk_exp[s], qk_exp.at(at.c, j + 1))
                dve.wait_ge(qkv_in[s], qkv_in.at(at.c, 5 + j))
                w, q, v = slot[s][:, j, :], slot[s][:, 2 + j, :], slot[s][:, 4 + j, :]
                sum_wv, sum_w = slot[s][:, 6 + j, :], slot[s][:, 8 + j, :]
                dve.tensor_tensor(v, v, w, ALU.mult).then_inc(own_v[s], own_v.one(s))
                dve.wait_ge(own_v[s], own_v.last(s, at.c))
                dve.tensor_tensor_scan(sum_wv, v, zero[:].to_broadcast([P, N]), carry0[s][:, j:j + 1], ALU.add, ALU.add).then_inc(own_v[s], own_v.one(s))
                dve.tensor_tensor_scan(sum_w, w, zero[:].to_broadcast([P, N]), carry0[s][:, 2 + j:3 + j], ALU.add,
                                       ALU.add).then_inc(own_v[s], own_v.one(s))
                dve.wait_ge(own_v[s], own_v.last(s, at.c))
                dve.wait_ge(qk_exp[s], qk_exp.at(at.c, 3 + j))
                dve.scalar_tensor_tensor(out=q, in0=q, scalar=1.0, in1=sum_w, op0=ALU.add, op1=ALU.mult).then_inc(own_v[s], own_v.one(s))
                last = slot[s][:, 6 + j:10:2, N - 1]
                dve.tensor_copy(carry0[s][:, j:j + 3:2], last).then_inc(own_v[s], own_v.one(s))
                dve.wait_ge(own_v[s], own_v.last(s, at.c))
                dve.reciprocal(q, q).then_inc(den_ok[s], 1)

            def ln(at, s, n):
                if n == 0:
                    dve.wait_ge(x2[s], x2.at(at.c, 1))
                if n in (0, 3):
                    tiles = HT0 if n == 0 else HT1
                    dve.wait_ge(down_ok, at.tile(tiles - 1, name="f0" if n == 0 else "f1"))
                out = Place(at.region, at.it, "out", s, n)
                for h in range(2):
                    src = bank[h]
                    if n in (1, 2):
                        dve.wait_ge(full[out.bank(h)], out.filled(h))
                        src = bank[out.bank(h)]
                    z = tok[s][:, 2 * h:2 * h + 2, :]
                    dve.scalar_tensor_tensor(out=z, in0=src[:].rearrange("p (t d) -> p t d", d=D),
                                             scalar=IWS, in1=z, op0=ALU.mult, op1=ALU.add).then_inc(own_v[s], own_v.one(s))
                dve.wait_ge(own_v[s], own_v.last(s, at.c))
                for t in range(TT):
                    ins = dve.bn_stats(bn[s][:, t, :], tok[s][:, t, :])
                ins.then_inc(own_v[s], own_v.one(s))
                dve.wait_ge(own_v[s], own_v.last(s, at.c))
                pause(s)
                for t in range(TT):
                    ins = dve.bn_aggr(mv[s][:, t, :], bn[s][:, t, :])
                ins.then_inc(var[s], 1)

            def norm(at, s, n):
                dve.wait_ge(rstd[s], rstd.at(at.c, n + 2))
                for t in range(TT):
                    v = tok[s][:, t, :]
                    ins = dve.tensor_scalar(v, v, mv[s][:, t, 0:1], stat[s][:, 2, t:t + 1], ALU.subtract, ALU.mult)
                ins.then_inc(normed[s], 1)

            def route(at, s, m):
                e = E0 if m == 0 else E1
                dve.wait_ge(full[at.bank()], at.filled())
                src = bank[at.bank()][:, 0:TT * G].rearrange("p (t g) -> p t g", g=G)[:, :, 0:e]
                lg = logit[s][:, m, :, :]
                if m == 0:
                    ins = dve.scalar_tensor_tensor(out=lg[:, :, 0:e], in0=src, scalar=IWS,
                                                   in1=smc("b_router").unsqueeze(1).to_broadcast([P, TT, E0]),
                                                   op0=ALU.mult, op1=ALU.add)
                else:
                    ins = dve.tensor_scalar(lg[:, :, 0:e], src, IWS, None, ALU.mult)
                ins.then_inc(logits[s], 1)
                dve.wait_ge(logits[s], logits.at(at.c, m + 1))
                pause(s)
                for t in range(TT):
                    ins = dve.max(top8[s][:, t, :], lg[:, t, :])
                ins.then_inc(own_v[s], own_v.one(s))
                dve.wait_ge(own_v[s], own_v.last(s, at.c))
                dve.tensor_tensor(prob[s][:], lg, top8[s][:, :, 0:1].to_broadcast([P, TT, G]),
                                  ALU.subtract).then_inc(soft_in[s], 1)
                for t in range(TT):
                    ins = dve.max_index(idx8[s][:, t, :], top8[s][:, t, :], lg[:, t, :])
                ins.then_inc(own_v[s], own_v.one(s))
                dve.wait_ge(own_v[s], own_v.last(s, at.c))
                num = iota[:].unsqueeze(1).to_broadcast([P, TT, G])
                for j in range(2):
                    dve.tensor_tensor(mask[s][:, j, :, :], num,
                                      idx8[s][:, :, j:j + 1].to_broadcast([P, TT, G]), ALU.is_equal).then_inc(own_v[s], own_v.one(s))
                dve.wait_ge(own_v[s], own_v.last(s, at.c))
                dve.tensor_tensor(mask[s][:, 0, :, :], mask[s][:, 0, :, :], mask[s][:, 1, :, :],
                                  ALU.add).then_inc(own_v[s], own_v.one(s))
                dve.wait_ge(own_v[s], own_v.last(s, at.c))

            def soft(at, s, m):
                dve.wait_ge(soft_exp[s], soft_exp.at(at.c, m + 1))
                st = sm_stat[s]
                pr = prob[s][:]
                dve.tensor_reduce(st[:, 0, :], pr, AX_X, ALU.add).then_inc(own_v[s], own_v.one(s))
                dve.wait_ge(own_v[s], own_v.last(s, at.c))
                dve.reciprocal(st[:, 1, :], st[:, 0, :]).then_inc(own_v[s], own_v.one(s))
                dve.wait_ge(own_v[s], own_v.last(s, at.c))
                dve.tensor_tensor(pr, pr, st[:, 1, :].unsqueeze(2).to_broadcast([P, TT, G]),
                                  ALU.mult).then_inc(own_v[s], own_v.one(s))
                dve.wait_ge(own_v[s], own_v.last(s, at.c))
                if m == 0:
                    dve.tensor_tensor(small8[s][:], pr, mask[s][:, 0, :, :], ALU.mult).then_inc(own_v[s], own_v.one(s))
                    dve.wait_ge(own_v[s], own_v.last(s, at.c))
                    dve.memset(small8[s][:, :, E0:E0 + 1], 1.0).then_inc(own_v[s], own_v.one(s))
                    dve.wait_ge(own_v[s], own_v.last(s, at.c))
                    return
                dve.tensor_tensor(pr, pr, mask[s][:, 0, :, :], ALU.mult).then_inc(own_v[s], own_v.one(s))
                dve.wait_ge(own_v[s], own_v.last(s, at.c))
                dve.tensor_reduce(st[:, 2, :], pr, AX_X, ALU.add).then_inc(own_v[s], own_v.one(s))
                dve.wait_ge(own_v[s], own_v.last(s, at.c))
                dve.tensor_scalar(st[:, 2, :], st[:, 2, :], 1e-20, None, ALU.add).then_inc(own_v[s], own_v.one(s))
                dve.wait_ge(own_v[s], own_v.last(s, at.c))
                dve.reciprocal(st[:, 1, :], st[:, 2, :]).then_inc(own_v[s], own_v.one(s))
                dve.wait_ge(own_v[s], own_v.last(s, at.c))
                dve.tensor_tensor(small8[s][:], pr,
                                  st[:, 1, :].unsqueeze(2).to_broadcast([P, TT, G]), ALU.mult).then_inc(own_v[s], own_v.one(s))
                dve.wait_ge(own_v[s], own_v.last(s, at.c))

            def hw(at, s, i):
                dve.wait_ge(full[at.bank()], at.filled())
                src = bank[at.bank()]
                dve.wait_ge(h_in[s], h_in.at(at.c, 1))
                v = slot[s][0:HL, 0, :]
                dve.tensor_tensor(v, v, src[0:HL, :], ALU.mult).then_inc(hw_ok[s], 1)

            def pjs(at, s, j):
                dve.wait_ge(tap0[s], tap0.at(at.c, j + 1))
                v = slot[s][:, j, :]
                for k in range(1, DCONV):
                    ins = dve.scalar_tensor_tensor(out=v, in0=pj[s][:, j, k:k + N],
                                                   scalar=smc("conv_w", j * DCONV + k, 1), in1=v, op0=ALU.mult,
                                                   op1=ALU.add)
                    if k < DCONV - 1:
                        ins.then_inc(own_v[s], own_v.one(s))
                        dve.wait_ge(own_v[s], own_v.last(s, at.c))
                ins.then_inc(conv_ok[s], 1)
                if j == CT - 1:
                    dve.tensor_copy(pj[s][:, :, 0:HIST], pj[s][:, :, N:N + HIST]).then_inc(hist_ok[s], 1)

            def dts(at, s, i):
                dve.wait_ge(full[at.bank()], at.filled())
                src = bank[at.bank()][:, 0:TT * G].rearrange("p (t g) -> p t g", g=G)
                d, m = dtb[s][:, 0, :, :], dtb[s][:, 1, :, :]
                dve.tensor_tensor(d, src, smc("dt_b").unsqueeze(1).to_broadcast([P, TT, NH]),
                                  ALU.add).then_inc(own_v[s], own_v.one(s))
                dve.wait_ge(own_v[s], own_v.last(s, at.c))
                dve.scalar_tensor_tensor(out=m, in0=d, scalar=-1.0, in1=d, op0=ALU.mult,
                                         op1=ALU.min).then_inc(dt_abs[s], 1)

            def softplus(at, s, i):
                dve.wait_ge(dt_ln[s], dt_ln.at(at.c, 1))
                dve.scalar_tensor_tensor(out=small8[s][:], in0=dtb[s][:, 0, :, :], scalar=0.0,
                                         in1=dtb[s][:, 1, :, :], op0=ALU.max, op1=ALU.add).then_inc(own_v[s], own_v.one(s))
                dve.wait_ge(own_v[s], own_v.last(s, at.c))

            def ct(at, s, j):
                X, drive = slot[s][:, j, :], slot[s][:, 6 + j % 2, :]
                dve.wait_ge(full[at.bank("dtx")], at.filled("dtx"))
                src = bank[at.bank("dtx")]
                dve.wait_ge(decay_ok[s], decay_ok.at(at.c, j + 1))
                dve.scalar_tensor_tensor(out=drive, in0=src[:], scalar=BC[:, j:j + 1], in1=X, op0=ALU.mult,
                                         op1=ALU.mult).then_inc(drive_ok[s], 1)
                dve.wait_ge(drive_ok[s], drive_ok.at(at.c, j + 1))
                dve.tensor_tensor_scan(drive, slot[s][:, 4 + j % 2, :], drive,
                                       carry1[s][:, j:j + 1], ALU.mult, ALU.add).then_inc(own_v[s], own_v.one(s))
                dve.wait_ge(own_v[s], own_v.last(s, at.c))
                dve.tensor_copy(carry1[s][:, j:j + 1], drive[:, N - 1:N])
                dve.scalar_tensor_tensor(out=X, in0=X, scalar=Dh[:, j:j + 1], in1=drive,
                                         op0=ALU.mult, op1=ALU.add).then_inc(own_v[s], own_v.one(s))
                dve.wait_ge(own_v[s], own_v.last(s, at.c))
                dve.wait_ge(tanh_ok[s], tanh_ok.at(at.c, j + 1))
                dve.scalar_tensor_tensor(out=X, in0=slot[s][:, 8 + j % 2, :], scalar=1.0, in1=X, op0=ALU.add,
                                         op1=ALU.mult).then_inc(comb_ok[s], 1)

            def swiglu(at, s, i):
                one = at.name == "f1"
                if i >= (HT1 if one else HT0):
                    return
                m = min(P, HID - i * P) if one else P
                dve.wait_ge(silu_ok, at.tile(i))
                dve.wait_ge(h_hi, at.tile(i, 2))
                dve.wait_ge(h_lo, at.tile(i, 2))
                r = (at.number(i)) % 2
                h = h32[0:m, r, :]
                dve.wait_ge(full[at.bank("u")], at.filled("u"))
                ins = dve.scalar_tensor_tensor(out=h, in0=bank[at.bank("u")][0:m, :], scalar=IWS, in1=sg[0:m, r, :],
                                               op0=ALU.mult, op1=ALU.mult)
                if one and i < RT:
                    ins.then_inc(own_v[s], own_v.one(s))
                    dve.wait_ge(own_v[s], own_v.last(s, at.c))
                    dve.wait_ge(full[at.bank("cw")], at.filled("cw"))
                    ins = dve.tensor_tensor(h, h, bank[at.bank("cw")][0:m, :], ALU.mult)
                ins.then_inc(h_ok, 1)

            dve.sem_inc(h_ok, 1)
            dve.memset(ones[:], 1.0)
            dve.memset(eps[:, 0, :], EPS_RMS)
            dve.memset(eps[:, 1, :], EPS_LN)
            dve.memset(neghalf[:], -0.5)
            dve.memset(hwh[:], 1.0)
            dve.memset(hwl[:], 0.0)
            dve.memset(zero[:], 0.0)
            for s in range(B):
                dve.memset(small8[s][:], 0.0)
                dve.memset(logit[s][:], NEG)
                dve.memset(carry0[s][:, 0:KD], 0.0)
                dve.memset(carry0[s][:, KD:], 1e-06)
                dve.memset(carry1[s][:], 0.0)
            dve.wait_ge(consts_in, 32)
            stage = slot[1][:, 0:5, :].rearrange("p a n -> p (a n)")
            dve.tensor_copy(ident[:], stage[:, 0:P])
            dve.tensor_copy(identb[:], stage[:, 0:P])
            dve.tensor_copy(iota[:], stage[:, P:P + G])
            dve.tensor_copy(sel[:], stage[:, P + G:C_COLS]).then_inc(consts_ok, 1)
            dve.scalar_tensor_tensor(out=BC[:], in0=smc("Bp"), scalar=0.5, in1=smc("Cp"), op0=ALU.mult, op1=ALU.mult)
            dve.tensor_scalar(Dh[:], smc("Dp"), 0.5, None, ALU.mult)
            dve.wait_ge(prep_a, 1)
            dve.tensor_scalar(negA[:], negA[:], -1.0, None, ALU.mult).then_inc(prep_v, 1)
            walk(dve, dict(piece=piece, xn=xn, T=T, sumsq=sumsq, spread=spread, qkn=qkn, cum=cum, ln=ln, norm=norm,
                           route=route, soft=soft, hw=hw, pj=pjs, dt=dts, softplus=softplus, ct=ct, f0=swiglu,
                           f1=swiglu))

        @block.gpsimd
        def _(pool):
            def pause(s):
                pool.tensor_tensor(idle[:, B + s:B + s + 1], ones[:], ones[:], ALU.mult)

            def rms(at, s, i):
                own_p.start(s)
                pool.wait_ge(normed[s], normed.at(at.c, 0))
                pool.wait_ge(squares[s], squares.at(at.c, 1))
                st = stat[s]
                pool.tensor_tensor(st[:, 1, :], st[:, 0, :], eps[:, 0, :], ALU.add).then_inc(own_p[s], own_p.one(s))
                pool.wait_ge(own_p[s], own_p.last(s, at.c))
                pool.tensor_tensor(st[:, 2, :], st[:, 1, :], neghalf[:, 0:TT], ALU.pow).then_inc(rstd[s], 1)

            def double(at, s, i):
                pool.wait_ge(stored[s], stored.at(at.c, 0))
                pool.wait_ge(x_in[s], x_in.at(at.c, 16))
                pause(s)
                pool.tensor_scalar(tok[s][:], xin[s], 2.0, 1.0, ALU.mult, ALU.mult).then_inc(x2[s], 1)

            def rqk(at, s, i):
                pool.wait_ge(ms_qk[s], ms_qk.at(at.c, 1))
                half = neghalf[:].rearrange("p (t g) -> p t g", g=G)[:, :, 0:2]
                pool.tensor_tensor(small8[s][:, :, 0:2], rest[s][:, :, 0:2], half, ALU.pow).then_inc(rqk_ok[s], 1)

            def y(at, s, j):
                pool.wait_ge(den_ok[s], den_ok.at(at.c, j + 1))
                v = slot[s][:, 2 + j, :]
                pool.tensor_tensor(v, v, slot[s][:, 6 + j, :], ALU.mult).then_inc(y_ok[s], 1)
                pool.wait_ge(c_hi[s], c_hi.at(at.c, j + 1))
                pool.tensor_tensor(cTl[s][:, j, :], v, cTh[s][:, j, :], ALU.subtract).then_inc(c_lo[s], 1)

            def ln(at, s, n):
                pool.wait_ge(var[s], var.at(at.c, n + 1))
                st = stat[s]
                pool.tensor_tensor(st[:, 1, :], mv[s][:, :, 1], eps[:, 1, :], ALU.add).then_inc(own_p[s], own_p.one(s))
                pool.wait_ge(own_p[s], own_p.last(s, at.c))
                pool.tensor_tensor(st[:, 2, :], st[:, 1, :], neghalf[:, 0:TT], ALU.pow).then_inc(rstd[s], 1)

            def hw(at, s, i):
                pool.wait_ge(hw_hi[s], hw_hi.at(at.c, 1))
                pool.tensor_tensor(hwl[0:HL, :], slot[s][0:HL, 0, :], hwh[0:HL, :],
                                   ALU.subtract).then_inc(hw_lo[s], 1)

            def comb(at, s, j):
                pool.wait_ge(c_hi[s], c_hi.at(at.c, 3 + j))
                pool.tensor_tensor(cTl[s][:, j, :], slot[s][:, j, :], cTh[s][:, j, :],
                                   ALU.subtract).then_inc(c_lo[s], 1)

            def swiglu(at, s, i):
                j = i - 1
                if not 0 <= j < (HT1 if at.name == "f1" else HT0):
                    return
                m = min(P, HID - j * P) if at.name == "f1" else P
                pool.wait_ge(h_hi, at.tile(j))
                n = at.number(j)
                pool.tensor_tensor(hTl[0:m, n % HR, :], h32[0:m, n % 2, :], hTh[0:m, n % HR, :],
                                   ALU.subtract).then_inc(h_lo, 1)

            pool.sem_inc(h_lo, 1)
            pool.wait_ge(consts_ok, 1)
            walk(pool, dict(rms=rms, double=double, rqk=rqk, y=y, ln=ln, hw=hw, comb=comb, f0=swiglu,
                             f1=swiglu))


def _rows(w):
    k, m = w.shape
    t = -(-k // P)
    full = np.zeros((t * P, m), w.dtype)
    full[:k] = w
    return full.reshape(t, P, m).transpose(1, 0, 2).reshape(P, t * m)


def _laid_out(i):
    qkv = i["L0_attn_w_qkv"].T
    parts = {
        "qkv": _rows(np.concatenate([qkv[:, D:2 * D], qkv[:, :D], qkv[:, 2 * D:]], 1)),
        "swi": _rows(i["L0_attn_w_swiglu"].T),
        "wo": _rows(i["L0_attn_w_out"].T),
        "lora_a": _rows(np.concatenate([i["L0_ffn_A_r"].transpose(1, 0, 2).reshape(D, ER), i["L0_ffn_A_s"]], 1)),
        "route0": _rows(i["L0_ffn_W_router"]),
        "base": _rows(i["L0_ffn_W_base"]),
        "lora_b": _rows(np.concatenate([i["L0_ffn_B_r"].reshape(ER, D), i["L0_ffn_B_s"],
                                        i["L0_ffn_b_base"][None]], 0)),
        "inp": _rows(i["L1_attn_in_proj_w"].T),
        "gatep": _rows(i["L1_attn_gate_proj_w"].T),
        "outp": _rows(i["L1_attn_out_proj_w"].T),
        "route1": _rows(i["L1_ffn_gate_weight"].T),
        "eg": _rows(np.concatenate([i["L1_ffn_w_gate"].reshape(-1, D), i["L1_ffn_sw_gate"]], 0).T),
        "eu": _rows(np.concatenate([i["L1_ffn_w_up"].reshape(-1, D), i["L1_ffn_sw_up"]], 0).T),
        "ed": _rows(np.concatenate([i["L1_ffn_w_down"].transpose(0, 2, 1).reshape(-1, D), i["L1_ffn_sw_down"].T], 0)),
    }
    wpack = np.concatenate([parts[n] for n, _ in W_PARTS], 1)

    def per_channel(v):
        return v.reshape(CT, P, -1).transpose(1, 0, 2).reshape(P, -1)

    dt_w = np.zeros((CT, P, NH), np.float32)
    for h in range(NH):
        c = h * (INNER // NH)
        dt_w[c // P, c % P:c % P + INNER // NH, h] = i["L1_attn_dt_w"][h]
    sparts = {
        "conv_w": per_channel(i["L1_attn_conv_w"]), "conv_b": per_channel(i["L1_attn_conv_b"]),
        "A_log": per_channel(i["L1_attn_A_log"]), "Bp": per_channel(i["L1_attn_Bp"]),
        "Cp": per_channel(i["L1_attn_Cp"]), "Dp": per_channel(i["L1_attn_Dp"]),
        "dt_b": np.broadcast_to(i["L1_attn_dt_b"], (P, NH)),
        "dt_w": dt_w.transpose(1, 0, 2).reshape(P, CT * NH),
        "b_router": np.broadcast_to(i["L0_ffn_b_router"], (P, E0)),
    }
    small = np.concatenate([sparts[n] for n, _ in S_PARTS], 1)
    return {"in_x_dram": i["L0_attn_x"], "in_wpack_dram": wpack, "in_small_dram": small,
            "in_const_dram": constants()}


def kernel(**inputs):
    import concourse.bacc as _bacc
    from concourse.bass_utils import run_bass_kernel_spmd as _run

    nc = _bacc.Bacc("TRN2", target_bir_lowering=False, num_devices=1)
    arrays = _laid_out({n: np.ascontiguousarray(a) for n, a in inputs.items()})
    arrays = {n: np.ascontiguousarray(a) for n, a in arrays.items()}
    args = [nc.dram_tensor(n, a.shape, mybir.dt.from_np(a.dtype), kind="ExternalInput").ap()
            for n, a in arrays.items()]
    args.append(nc.dram_tensor("out_0_dram", (B, S, D), F32, kind="ExternalOutput").ap())
    nc.disable_value_cache = True
    bass_two_postnorm_layers(nc, *args)
    r = _run(nc, [arrays], core_ids=[0])
    return r.results[0]["out_0_dram"]
```

```python
from contextlib import ExitStack

import numpy as np
import concourse.bass as bass
from concourse import mybir

ALU = mybir.AluOpType
ACT = mybir.ActivationFunctionType
F32 = mybir.dt.float32
F16 = mybir.dt.float16
BF16 = mybir.dt.bfloat16
U32 = mybir.dt.uint32
AX_X = mybir.AxisListType.X

P = 128
B, S, D = 2, 2048, 256
N = 512
CH = S // N
TT = N // P
KD = D // P
DFF = 1024
E0, R0 = 6, 16
ER = E0 * R0
HL = ER + E0 + R0
INNER, NH, DCONV = 512, 8, 4
CT = INNER // P
E1, F1, FS = 8, 176, 352
HID = E1 * F1 + FS
M0 = FS % P
SH = -(-FS // P)
RT = E1 * F1 // P
EPS_RMS, EPS_LN = 1.1920929e-07, 1e-05
WS = 256.0
IWS = 1.0 / WS
G = 8
NEG = -3.0e38
HT0 = DFF // P
HT1 = SH + RT
NB, NBL = 4, 2
HR = 4

W_PARTS = [("qkv", KD * 3 * D), ("swi", KD * 2 * DFF), ("wo", HT0 * D), ("lora_a", KD * HL),
           ("base", KD * D), ("lora_b", D), ("inp", KD * INNER), ("gatep", KD * INNER), ("outp", CT * D),
           ("eg", KD * (HID + E1)), ("eu", KD * HID), ("ed", HT1 * D)]
W_AT = {}
W_COLS = 0
for _n, _c in W_PARTS:
    W_AT[_n] = (W_COLS, _c)
    W_COLS += _c
PIECES = 11
PC = -(-W_COLS // PIECES)
S_PARTS = [("conv_w", CT * DCONV), ("conv_b", CT), ("A_log", CT), ("Bp", CT), ("Cp", CT), ("Dp", CT), ("dt_b", CT),
           ("dt_w", CT * P), ("b_router", E0)]
S_AT = {}
S_COLS = 0
for _n, _c in S_PARTS:
    S_AT[_n] = (S_COLS, _c)
    S_COLS += _c
C_PARTS = [("ident", P), ("iota", G), ("sel_q", 2 * P), ("sel_g", HL), ("sel_cw", RT * P)]
C_AT = {}
C_COLS = 0
for _n, _c in C_PARTS:
    C_AT[_n] = (C_COLS, _c)
    C_COLS += _c


def constants():
    c = np.zeros((P, C_COLS), np.float32)
    c[:, :P] = np.eye(P, dtype=np.float32)
    c[:, C_AT["iota"][0]:C_AT["iota"][0] + G] = np.arange(G, dtype=np.float32)

    def put(name, k, width, column_of):
        for m in range(width):
            for part in range(3):
                c[part * G + column_of(m), C_AT[name][0] + k * width + m] = 1.0

    for j in range(2):
        put("sel_q", j, P, lambda m: j)
    put("sel_g", 0, HL, lambda m: min(m // R0, E0))
    for j in range(RT):
        put("sel_cw", j, P, lambda m: (P * j + m) // F1)
    return c


def light1(s):
    return ([("rms", s, 0), ("xn", s, 0), ("double", s, 0), ("T", s, 0)] + [("qkv", s, j) for j in range(6)]
            + [("sumsq", s, 0), ("rqk", s, 0), ("spread", s, 0), ("qkn", s, 0), ("qkn", s, 1),
               ("cum", s, 0), ("cum", s, 1), ("y", s, 0), ("y", s, 1)])


def light2(s, more):
    return ([("ln", s, 0), ("norm", s, 0), ("T", s, 1), ("h112", s, 0), ("route", s, 0), ("soft", s, 0),
             ("spread", s, 1), ("hw", s, 0), ("out", s, 1), ("ln", s, 1), ("norm", s, 1), ("T", s, 2)]
            + [("pj", s, 0)] + [x for j in range(1, CT) for x in (("pj", s, j), ("silu", s, j - 1))]
            + [("silu", s, CT - 1)] + [("dt", s, j) for j in range(CT)] + [("softplus", s, j) for j in range(CT)]
            + [("ct", s, 0)]
            + [x for j in range(1, CT) for x in (("ct", s, j), ("comb", s, j - 1))] + [("comb", s, CT - 1)] + [("load", s, 0)] * more
            + [("out", s, 2), ("ln", s, 2), ("norm", s, 2), ("T", s, 3)])


def ffn0(s):
    return [("f0", s, i) for i in range(HT0 + 2)]


def ffn1(s):
    f = [("f1", s, i) for i in range(HT1 + 2)]
    return f[:1] + [("route", s, 1)] + f[1:2] + [("soft", s, 1)] + f[2:3] + [("spread", s, 2)] + f[3:]


def end(s):
    return [("ln", s, 3), ("norm", s, 3), ("store", s, 0)]


def merge(runs, *chains):
    out, done = [], [0, 0]
    for k, n in enumerate(runs):
        out += chains[k % 2][done[k % 2]:done[k % 2] + n]
        done[k % 2] += n
    assert done == [len(c) for c in chains], (done, [len(c) for c in chains])
    return out


def round_of(runs, more):
    return merge(runs, ffn0(0) + light2(0, more) + ffn1(0) + end(0) + (light1(0) if more else []),
                 light1(1) + ffn0(1) + light2(1, more) + ffn1(1) + end(1))


def with_pieces(order, after):
    out = []
    for k, step in enumerate(order):
        out.append(step)
        out += [("piece", 0, j) for j in after if after[j] == k + 1]
    return out


RUNS = {"body": [0, 1, 3, 1, 3, 2, 3, 1, 2, 1, 1, 5, 2, 2, 1, 1, 1, 1, 1, 1, 2, 3, 2, 2, 1, 1, 4, 1, 3, 1, 4, 1, 1,
                 3, 1, 2, 2, 1, 4, 1, 4, 1, 1, 2, 2, 1, 2, 1, 1, 2, 1, 1, 1, 1, 2, 7, 2, 3, 1, 1, 1, 1, 1, 1, 2, 4,
                 1, 1, 1, 2, 1, 2, 4, 1, 1, 1, 1, 1, 3, 2, 2, 1, 1, 1, 1, 1, 1, 2, 1, 1, 5, 1, 1, 1, 1, 3, 1, 2, 1,
                 2, 2, 2, 1, 7],
        "epi": [0, 1, 2, 1, 3, 1, 1, 1, 5, 5, 4, 2, 2, 2, 1, 2, 1, 3, 2, 1, 1, 1, 4, 1, 2, 2, 4, 2, 3, 3, 2, 1, 1,
                2, 1, 1, 3, 4, 1, 1, 1, 1, 3, 2, 1, 1, 2, 1, 1, 2, 1, 3, 1, 2, 2, 1, 1, 1, 1, 2, 2, 4, 1, 2, 1, 3,
                1, 1, 2, 2, 1, 2, 1, 1, 2, 3, 2, 5, 1, 10, 1, 5]}
PRO = ([("load", 0, 0), ("consts", 0, 0), ("fetch", 0, 0), ("load", 1, 0), ("fetch", 0, 1)] + light1(0)[:2] + [("prep", 0, 0)]
       + light1(0)[2:])
SCHEDULE = {"pro": with_pieces(PRO, {0: 9, 1: 14, 2: 18}),
            "first": with_pieces(round_of(RUNS["body"], True), {3: 1, 4: 4, 5: 6, 6: 8, 7: 13, 8: 18, 9: 36, 10: 41}),
            "body": round_of(RUNS["body"], True), "epi": round_of(RUNS["epi"], False)}
REGIONS = ("pro", "first", "body", "epi")


def tiles_of(name, i):
    if name == "T":
        return [(k, "light") for k in range(KD)]
    if name in ("qkv", "sumsq", "spread", "qkn", "route", "h112", "hw", "pj", "dt"):
        return [(0, "light")]
    if name == "ct":
        return [("gate", "light")]
    if name == "out":
        return [(0, "light"), (1, "light")]
    if name in ("f0", "f1"):
        t = [(0, 0), (1, 1)] if i == 2 else []
        n = HT0 if name == "f0" else HT1
        if i < n:
            t += [("g", "hidden"), ("u", "hidden")]
            if name == "f1" and i >= SH:
                t.append(("cw", "hidden"))
        return t
    return []


class Banks:

    def __init__(self):
        self.place, self.totals, self.base, self.last = {}, {}, {}, {}
        before = {b: 0 for b in range(8)}
        for region in REGIONS:
            used = {b: 0 for b in range(8)}
            last = {}
            ring = {"hidden": 0, "light": 0}
            for name, s, i in SCHEDULE[region]:
                for tile, where in tiles_of(name, i):
                    if where == "hidden":
                        b = 2 + ring[where] % NB
                    elif where == "light":
                        b = 2 + NB + ring[where] % NBL
                    else:
                        b = where
                    if where in ring:
                        ring[where] += 1
                    self.place[region, name, s, i, tile] = (b, used[b], last.get(b))
                    last[b] = (name, s, i, tile)
                    used[b] += 1
            self.totals[region], self.base[region], self.last[region] = used, dict(before), last
            times = CH - 2 if region == "body" else 1
            before = {b: before[b] + times * used[b] for b in range(8)}


def hidden_index():
    first, n = {}, {}
    for region in SCHEDULE:
        n[region] = 0
        for name, s, i in SCHEDULE[region]:
            if name in ("f0", "f1") and i == 0:
                first[region, name, s] = n[region]
                n[region] += HT0 if name == "f0" else HT1
    return first, n["body"]


class Signal:

    def __init__(self, sem, name, per):
        self.name, self.per = name, per
        self.sems = [sem(f"{name}{s}") for s in range(B)]
        self.n = [0] * B

    def __getitem__(self, s):
        return self.sems[s]

    def at(self, c, j):
        it, ahead = c
        return it * self.per + (ahead * self.per + j)

    def start(self, s):
        assert self.n[s] in (0, self.per), (self.name, self.n)
        self.n[s] = 0

    def one(self, s):
        self.n[s] += 1
        return 1

    def last(self, s, c):
        return self.at(c, self.n[s])


def bass_two_postnorm_layers(nc, x, wpack, small, const, out):
    banks = Banks()
    hidden_first, HB = hidden_index()
    assert HB % HR == 0

    with ExitStack() as ctx:
        def sb(name, shape, dt=F32):
            return ctx.enter_context(nc.sbuf_tensor(name, shape, dt))

        def sem(name):
            return ctx.enter_context(nc.semaphore(name))

        def sems(name):
            return [sem(f"{name}{s}") for s in range(B)]

        bank = [ctx.enter_context(nc.psum_tensor(f"bank{b}", [P, N], F32)) for b in range(8)]

        Wh, Wl = sb("Wh", [P, W_COLS], F16), sb("Wl", [P, W_COLS], F16)
        sm = sb("sm", [P, S_COLS])
        ident = sb("ident", [P, P])
        identb = sb("identb", [P, P], BF16)
        iota = sb("iota", [P, G])
        sel = sb("sel", [P, C_COLS - P - G], BF16)
        zero = sb("zero", [P, 1])
        ones = sb("ones", [P, 1])
        eps = sb("eps", [P, 2, TT])
        idle = sb("idle", [P, 2 * B])
        neghalf = sb("neghalf", [P, TT * G])
        BC = sb("BC", [P, CT])
        Dh = sb("Dh", [P, CT])
        negA = sb("negA", [P, CT])
        tok = [sb(f"tok{s}", [P, TT, D]) for s in range(B)]
        xTh = [sb(f"xTh{s}", [P, KD, N], F16) for s in range(B)]
        xTl = [sb(f"xTl{s}", [P, KD, N], F16) for s in range(B)]
        slot = [sb(f"slot{s}", [P, 10, N]) for s in range(B)]
        xin = [slot[s][:, 8:10, :].rearrange("p a (t d) -> p (a t) d", d=D) for s in range(B)]
        cTh = [sb(f"cTh{s}", [P, CT, N], F16) for s in range(B)]
        cTl = [sb(f"cTl{s}", [P, CT, N], F16) for s in range(B)]
        hwh, hwl = sb("hwh", [P, N], F16), sb("hwl", [P, N], F16)
        HIST = DCONV - 1
        pj = [sb(f"pj{s}", [P, CT, HIST + N]) for s in range(B)]
        partsT = [sb(f"partsT{s}", [3 * G, N], BF16) for s in range(B)]
        small8 = [sb(f"small8{s}", [P, TT, G]) for s in range(B)]
        rest = [sb(f"rest{s}", [P, TT, G]) for s in range(B)]
        parts = [sb(f"parts{s}", [P, TT, 3, G], BF16) for s in range(B)]
        logit = [sb(f"logit{s}", [P, 2, TT, G]) for s in range(B)]
        top8 = [sb(f"top8{s}", [P, TT, G]) for s in range(B)]
        idx8 = [sb(f"idx8{s}", [P, TT, G], U32) for s in range(B)]
        mask = [sb(f"mask{s}", [P, 2, TT, G]) for s in range(B)]
        prob = [sb(f"prob{s}", [P, TT, G]) for s in range(B)]
        stat = [sb(f"stat{s}", [P, 3, TT]) for s in range(B)]
        bn = [sb(f"bn{s}", [P, TT, 6]) for s in range(B)]
        mv = [sb(f"mv{s}", [P, TT, 2]) for s in range(B)]
        carry0 = [sb(f"carry0{s}", [P, 2 * KD]) for s in range(B)]
        carry1 = [sb(f"carry1{s}", [P, CT]) for s in range(B)]
        sg = sb("sg", [P, 2, N])
        h32 = sb("h32", [P, 2, N])
        hTh = sb("hTh", [P, HR, N], F16)
        hTl = sb("hTl", [P, HR, N], F16)

        sm_stat = [sb(f"sm_stat{s}", [P, 3, TT]) for s in range(B)]

        full = [sem(f"bank_full{b}") for b in range(8)]
        piece_in = [sem(f"piece_in{j}") for j in range(2)]
        consts_in, ident_ok, consts_ok = sem("consts_in"), sem("ident_ok"), sem("consts_ok")
        filled_ok = sem("filled_ok")
        piece_hi, piece_lo = sem("piece_hi"), sem("piece_lo")
        prep_a, prep_p, prep_v = sem("prep_a"), sem("prep_p"), sem("prep_v")
        silu_ok, h_ok = sem("silu_ok"), sem("h_ok")
        h_hi, h_lo, down_ok = sem("h_hi"), sem("h_lo"), sem("down_ok")

        x_in, stored = Signal(sem, "x_in", 16), Signal(sem, "stored", 16)
        squares = Signal(sem, "squares", 1)
        rstd = Signal(sem, "rstd", 5)
        var = Signal(sem, "var", 4)
        normed = Signal(sem, "normed", 5)
        x2 = Signal(sem, "x2", 1)
        xT_hi, xT_lo = Signal(sem, "xT_hi", 8), Signal(sem, "xT_lo", 8)
        qkv_in = Signal(sem, "qkv_in", 6)
        sq_in = Signal(sem, "sq_in", 4)
        sumsq_in = Signal(sem, "sumsq_in", 2)
        ms_qk, rqk_ok = Signal(sem, "ms_qk", 1), Signal(sem, "rqk_ok", 1)
        parts_ok = Signal(sem, "parts_ok", 3)
        partsT_ok = Signal(sem, "partsT_ok", 3)
        qk_normed = Signal(sem, "qk_normed", 4)
        qk_exp = Signal(sem, "qk_exp", 4)
        den_ok, y_ok = Signal(sem, "den_ok", 2), Signal(sem, "y_ok", 2)
        c_hi, c_lo = Signal(sem, "c_hi", 6), Signal(sem, "c_lo", 6)
        logits = Signal(sem, "logits", 2)
        soft_in, soft_exp = Signal(sem, "soft_in", 2), Signal(sem, "soft_exp", 2)
        g_in = Signal(sem, "g_in", 1)
        h_in, hw_ok = Signal(sem, "h_in", 1), Signal(sem, "hw_ok", 1)
        hw_hi, hw_lo = Signal(sem, "hw_hi", 1), Signal(sem, "hw_lo", 1)
        pj_in, tap0 = Signal(sem, "pj_in", 4), Signal(sem, "tap0", 4)
        conv_ok, X_ok = Signal(sem, "conv_ok", 4), Signal(sem, "X_ok", 4)
        dt_abs, dt_exp, dt_ln = Signal(sem, "dt_abs", 4), Signal(sem, "dt_exp", 4), Signal(sem, "dt_ln", 4)
        dt_pos, dt_ok = Signal(sem, "dt_pos", 4), Signal(sem, "dt_ok", 4)
        decay_ok, drive_ok = Signal(sem, "decay_ok", 4), Signal(sem, "drive_ok", 4)
        tanh_ok, comb_ok = Signal(sem, "tanh_ok", 4), Signal(sem, "comb_ok", 4)
        own_v = Signal(sem, "own_v", 81)
        own_p = Signal(sem, "own_p", 5)
        hist_ok = [sem(f"hist_ok{s}") for s in range(B)]

        def wcols(part, k, width, a=0, n=None):
            at = W_AT[part][0] + k * width + a
            n = width if n is None else n
            return Wh[:, at:at + n], Wl[:, at:at + n]

        def expert_cols(part, k, i):
            extra = E1 if part == "eg" else 0
            if i == 0:
                return wcols(part, k, HID + extra, 0, M0 + extra)
            return wcols(part, k, HID + extra, M0 + extra + (i - 1) * P, P)

        def rows_of(name, i):
            return M0 if name == "f1" and i == 0 else P

        def pieces_to(part):
            at, n = W_AT[part]
            return -(-(at + n) // PC)

        def selcols(part, k, width):
            at = C_AT[part][0] - P - G + k * width
            return sel[0:3 * G, at:at + width]

        def smc(part, a=0, n=None):
            at, w = S_AT[part]
            return sm[:, at + a:at + a + (w - a if n is None else n)]

        LIGHT1 = {"rms", "xn", "double", "qkv", "sumsq", "rqk", "qkn", "cum", "y"}

        def chunk(region, it, name, s, i):
            ahead = name == "load" or (s == 0 and (name in LIGHT1 or (name in ("T", "spread") and i == 0)))
            return (0, 0) if region == "pro" else (it, int(ahead))

        class Place:

            def __init__(self, region, it, name, s, i):
                self.region, self.it, self.name, self.s, self.i = region, it, name, s, i
                self.c = chunk(region, it, name, s, i)

            def bank(self, tile=0):
                return banks.place[self.region, self.name, self.s, self.i, tile][0]

            def filled(self, tile=0):
                b, n, _ = banks.place[self.region, self.name, self.s, self.i, tile]
                n += banks.base[self.region][b] + 1
                if self.region == "body":
                    per = banks.totals["body"][b]
                    return self.it * per + (n - per)
                return n

            def number(self, i, name=None):
                return hidden_first[self.region, name or self.name, self.s] + i

            def tile(self, i, back=0, name=None):
                n = self.number(i, name) - back + 1
                return self.it * HB + (max(n, 0) if self.region == "first" else n) + 1

            def used(self, tile=0):
                b, _, last = banks.place[self.region, self.name, self.s, self.i, tile]
                if last is not None:
                    return readers(self.region, self.it, last)
                before = {"pro": None, "first": "pro", "body": "body", "epi": "body"}[self.region]
                if before is None or b not in banks.last[before]:
                    return []
                return readers(before, self.it, banks.last[before][b], 1)

        def readers(region, it, tile, back=0):
            name, s, i, which = tile
            if which in ("g", "u", "cw"):
                n = hidden_first[region, name, s] + i + 2 - back * HB
                return [(silu_ok if which == "g" else h_ok, it * HB + n)]
            it, ahead = chunk(region, it, name, s, i)
            c = (it, ahead - back) if region != "pro" else (0, 0)
            if name == "T":
                found = [(xT_hi, 2 * i + which + 1), (xT_lo, 2 * i + which + 1)]
            elif name == "ct":
                found = [(tanh_ok, i + 1)]
            elif name in ("f0", "f1"):
                found = [(var, 1 if name == "f0" else 4)]
            else:
                found = [{"qkv": (qkv_in, i + 1), "sumsq": (ms_qk, 1), "spread": (partsT_ok, i + 1),
                          "qkn": (qk_normed, 2 * i + 2), "route": (logits, i + 1), "h112": (h_in, 1),
                          "hw": (hw_ok, 1), "out": (var, i + 1), "pj": (pj_in, i + 1), "dt": (dt_pos, i + 1)}[name]]
            return [(signal[s], signal.at(c, j)) for signal, j in found]

        def walk(engine, steps):
            for region in REGIONS:
                if region == "body":
                    with engine.Fori(1, CH - 1) as it:
                        for name, s, i in SCHEDULE[region]:
                            if name in steps:
                                steps[name](Place(region, it, name, s, i), s, i)
                else:
                    for name, s, i in SCHEDULE[region]:
                        if name in steps:
                            steps[name](Place(region, CH - 1 if region == "epi" else 0, name, s, i), s, i)

        block = ctx.enter_context(nc.Block())

        @block.sync
        def _(sp):
            def load(at, s, i):
                if at.region != "pro":
                    sp.wait_ge(comb_ok[s], comb_ok.at((at.it, 0), CT))
                src = x[s][bass.ds((at.c[0] + at.c[1]) * N, N), :].rearrange("(t p) d -> p t d", p=P)
                sp.dma_start(xin[s], src).then_inc(x_in[s], 16)

            def store(at, s, i):
                sp.wait_ge(normed[s], normed.at(at.c, 5))
                dst = out[s][bass.ds((at.c[0] + at.c[1]) * N, N), :].rearrange("(t p) d -> p t d", p=P)
                sp.dma_start(dst, tok[s][:]).then_inc(stored[s], 16)

            def fetch(at, s, j):
                a, n = j * PC, min(PC, W_COLS - j * PC)
                stage = pj[j % 2][:].rearrange("p a n -> p (a n)")
                sp.dma_start(stage[:, 0:n], wpack[:, a:a + n]).then_inc(piece_in[j % 2], 16)

            def piece(at, s, j):
                if j + 2 < PIECES:
                    sp.wait_ge(piece_hi, j + 1)
                    sp.wait_ge(piece_lo, j + 1)
                    fetch(at, s, j + 2)

            def consts(at, s, i):
                stage = slot[1][:, 0:5, :].rearrange("p a n -> p (a n)")
                sp.dma_start(stage[:, 0:C_COLS], const).then_inc(consts_in, 16)
                sp.dma_start(sm[:], small).then_inc(consts_in, 16)

            walk(sp, {"consts": consts, "load": load, "store": store, "fetch": fetch, "piece": piece})
            for s in range(B):
                sp.wait_ge(stored[s], stored.at((CH, 0), 0))

        @block.tensor
        def _(pe):
            def mm3(dst, lhs, rhs, first, last):
                pe.matmul(dst, lhs[0], rhs[0], start=first, stop=False, skip_group_check=True)
                pe.matmul(dst, lhs[0], rhs[1], start=False, stop=False, skip_group_check=True)
                return pe.matmul(dst, lhs[1], rhs[0], start=False, stop=last, skip_group_check=True)

            def weights(at, part):
                if at.region in ("pro", "first"):
                    pe.wait_ge(piece_hi, pieces_to(part))
                    pe.wait_ge(piece_lo, pieces_to(part))

            def xT(s, k, t=None):
                c = slice(0, N) if t is None else slice(t * P, (t + 1) * P)
                return xTh[s][:, k, c], xTl[s][:, k, c]

            def T(at, s, t):
                pe.wait_ge(normed[s], normed.at(at.c, t + 1))
                if at.region == "pro":
                    pe.wait_ge(ident_ok, 1)
                src = slot[s][:, 0:2, :].rearrange("p a (t d) -> p (a t) d", d=D) if t == 0 else tok[s]
                for k in range(KD):
                    for reader, n in at.used(k):
                        pe.wait_ge(reader, n)
                    b = at.bank(k)
                    for tt in range(TT):
                        mm = pe.transpose(bank[b][:, tt * P:(tt + 1) * P], src[:, tt, k * P:(k + 1) * P], ident[:])
                    mm.then_inc(full[b], 1)

            def project(at, tile, part, width, a, m, s):
                for reader, n in at.used(tile):
                    pe.wait_ge(reader, n)
                b = at.bank(tile)
                for k in range(KD):
                    mm = mm3(bank[b][0:m, :], wcols(part, k, width, a, m), xT(s, k), k == 0, k == KD - 1)
                mm.then_inc(full[b], 1)

            def qkv(at, s, j):
                if j == 0:
                    pe.wait_ge(xT_hi[s], xT_hi.at(at.c, 2))
                    pe.wait_ge(xT_lo[s], xT_lo.at(at.c, 2))
                    weights(at, "qkv")
                project(at, 0, "qkv", 3 * D, j * P, P, s)

            def sumsq(at, s, i):
                for reader, n in at.used():
                    pe.wait_ge(reader, n)
                b = at.bank()
                for j in range(2):
                    pe.wait_ge(sumsq_in[s], sumsq_in.at(at.c, j + 1))
                    for t in range(TT):
                        mm = pe.matmul(bank[b][:, t * G + j:t * G + j + 1], slot[s][:, 6 + 2 * j, t * P:(t + 1) * P],
                                       ones[:], start=True, stop=True)
                mm.then_inc(full[b], 1)

            def spread(at, s, e):
                for reader, n in at.used():
                    pe.wait_ge(reader, n)
                b = at.bank()
                pe.wait_ge(parts_ok[s], parts_ok.at(at.c, e + 1))
                dst = bank[b][:].bitcast(BF16)
                for t in range(TT):
                    src = parts[s][:, t, :, :].rearrange("p a g -> p (a g)")
                    mm = pe.transpose(dst[0:3 * G, t * P:(t + 1) * P], src, identb[:])
                mm.then_inc(full[b], 1)

            def select(at, tile, part, k, width, s, e):
                for reader, n in at.used(tile):
                    pe.wait_ge(reader, n)
                b = at.bank(tile)
                pe.wait_ge(partsT_ok[s], partsT_ok.at(at.c, e + 1))
                pe.matmul(bank[b][0:width, :], selcols(part, k, width), partsT[s][:], start=True,
                          stop=True).then_inc(full[b], 1)

            def qkn(at, s, j):
                select(at, 0, "sel_q", j, P, s, 0)

            def swiglu(at, s, i):
                one = at.name == "f1"
                tiles = HT1 if one else HT0
                if i == 0 and one:
                    pe.wait_ge(xT_hi[s], xT_hi.at(at.c, 8))
                    pe.wait_ge(xT_lo[s], xT_lo.at(at.c, 8))
                if i == 0 and not one:
                    pe.wait_ge(c_hi[s], c_hi.at(at.c, 2))
                    pe.wait_ge(c_lo[s], c_lo.at(at.c, 2))
                if i == 0:
                    weights(at, "ed" if one else "swi")
                if i < tiles:
                    for tile in ("g", "u"):
                        for reader, n in at.used(tile):
                            pe.wait_ge(reader, n)
                        b = at.bank(tile)
                        m = rows_of(at.name, i) + (E1 if one and i == 0 and tile == "g" else 0)
                        for k in range(KD):
                            if one:
                                w, rhs = expert_cols("e" + tile, k, i), xT(s, k)
                            else:
                                w = wcols("swi", k, 2 * DFF, (DFF if tile == "g" else 0) + i * P, m)
                                rhs = cTh[s][:, k, :], cTl[s][:, k, :]
                            mm = mm3(bank[b][0:m, :], w, rhs, k == 0, k == KD - 1)
                        mm.then_inc(full[b], 1)
                    if one and i >= SH:
                        select(at, "cw", "sel_cw", i - SH, P, s, 2)
                j = i - 2
                if j < 0:
                    return
                m = rows_of(at.name, j)
                if j == 0:
                    for reader, n in at.used(0):
                        pe.wait_ge(reader, n)
                    for reader, n in at.used(1):
                        pe.wait_ge(reader, n)
                    if not one:
                        weights(at, "wo")
                pe.wait_ge(h_hi, at.tile(j))
                pe.wait_ge(h_lo, at.tile(j))
                r = (at.number(j)) % HR
                wh, wl = wcols("ed" if one else "wo", j, D)
                for t in range(TT):
                    c = slice(t * P, (t + 1) * P)
                    mm = mm3(bank[t // 2][:, (t % 2) * D:(t % 2 + 1) * D], (hTh[0:m, r, c], hTl[0:m, r, c]),
                             (wh[0:m], wl[0:m]), j == 0 and t % 2 == 0, j == tiles - 1)
                mm.then_inc(down_ok, 1)

            def route(at, s, m):
                for reader, n in at.used():
                    pe.wait_ge(reader, n)
                b = at.bank()
                if m == 0:
                    pe.wait_ge(h_in[s], h_in.at(at.c, 1))
                else:
                    pe.wait_ge(g_in[s], g_in.at(at.c, 1))
                rows = HL if m == 0 else M0 + E1
                for t in range(TT):
                    mm = pe.transpose(bank[b][:, t * P:t * P + rows], slot[s][0:rows, 0, t * P:(t + 1) * P],
                                      ident[0:rows, 0:rows])
                mm.then_inc(full[b], 1)

            def h112(at, s, i):
                pe.wait_ge(xT_hi[s], xT_hi.at(at.c, 4))
                pe.wait_ge(xT_lo[s], xT_lo.at(at.c, 4))
                weights(at, "lora_a")
                project(at, 0, "lora_a", HL, 0, HL, s)

            def hw(at, s, i):
                select(at, 0, "sel_g", 0, HL, s, 1)

            def outp(at, s, m):
                weights(at, "lora_b" if m == 1 else "outp")
                for h in range(2):
                    for reader, n in at.used(h):
                        pe.wait_ge(reader, n)
                    b = at.bank(h)
                    if m == 1:
                        pe.wait_ge(hw_hi[s], hw_hi.at(at.c, 1))
                        pe.wait_ge(hw_lo[s], hw_lo.at(at.c, 1))
                    else:
                        pe.wait_ge(c_hi[s], c_hi.at(at.c, 6))
                        pe.wait_ge(c_lo[s], c_lo.at(at.c, 6))
                    for t in range(2 * h, 2 * h + 2):
                        dst = bank[b][:, (t % 2) * D:(t % 2 + 1) * D]
                        c = slice(t * P, (t + 1) * P)
                        if m == 1:
                            for k in range(KD):
                                mm3(dst, xT(s, k, t), wcols("base", k, D), k == 0, False)
                            wh, wl = wcols("lora_b", 0, D)
                            mm = mm3(dst, (hwh[0:HL + 1, c], hwl[0:HL + 1, c]), (wh[0:HL + 1], wl[0:HL + 1]),
                                     False, True)
                        else:
                            for k in range(CT):
                                mm = mm3(dst, (cTh[s][:, k, c], cTl[s][:, k, c]), wcols("outp", k, D), k == 0,
                                         k == CT - 1)
                    mm.then_inc(full[b], 1)

            def pjs(at, s, j):
                if j == 0:
                    pe.wait_ge(xT_hi[s], xT_hi.at(at.c, 6))
                    pe.wait_ge(xT_lo[s], xT_lo.at(at.c, 6))
                    weights(at, "inp")
                project(at, 0, "inp", INNER, j * P, P, s)

            def dts(at, s, j):
                for reader, n in at.used():
                    pe.wait_ge(reader, n)
                b = at.bank()
                pe.wait_ge(X_ok[s], X_ok.at(at.c, j + 1))
                pe.matmul(bank[b][:], smc("dt_w", j * P, P), slot[s][:, j, :], start=True, stop=True).then_inc(full[b], 1)

            def ct(at, s, j):
                weights(at, "gatep")
                project(at, "gate", "gatep", INNER, j * P, P, s)

            pe.sem_inc(down_ok, 1)
            walk(pe, {"T": T, "qkv": qkv, "sumsq": sumsq, "spread": spread, "qkn": qkn, "f0": swiglu, "f1": swiglu,
                      "route": route, "h112": h112, "hw": hw, "out": outp, "pj": pjs, "dt": dts, "ct": ct})

        @block.scalar
        def _(act):
            def piece(at, s, j):
                a, n = j * PC, min(PC, W_COLS - j * PC)
                act.wait_ge(piece_in[j % 2], 16 * (j // 2 + 1))
                stage = pj[j % 2][:].rearrange("p a n -> p (a n)")
                act.activation(Wh[:, a:a + n], stage[:, 0:n], ACT.Copy, scale=WS).then_inc(piece_hi, 1)

            def rms(at, s, i):
                act.wait_ge(x_in[s], x_in.at(at.c, 16))
                for t in range(TT):
                    ins = act.activation(slot[s][:, 2 + t, 0:D], xin[s][:, t, :], ACT.Square, scale=D ** -0.5,
                                         accum_out=stat[s][:, 0, t:t + 1])
                ins.then_inc(squares[s], 1)

            def T(at, s, t):
                for k in range(KD):
                    act.wait_ge(full[at.bank(k)], at.filled(k))
                    act.activation(xTh[s][:, k, :], bank[at.bank(k)][:], ACT.Copy).then_inc(xT_hi[s], 1)

            def qkv(at, s, j):
                act.wait_ge(full[at.bank()], at.filled())
                act.activation(slot[s][:, j, :], bank[at.bank()][:], ACT.Copy, scale=IWS).then_inc(qkv_in[s], 1)
                if j < 2 * KD:
                    if j == KD:
                        act.wait_ge(x2[s], x2.at(at.c, 1))
                    act.wait_ge(qkv_in[s], qkv_in.at(at.c, j + 1))
                    act.activation(slot[s][:, 6 + j, :], slot[s][:, j, :], ACT.Square).then_inc(sq_in[s], 1)

            def spread(at, s, e):
                act.wait_ge(full[at.bank()], at.filled())
                src = bank[at.bank()][:].bitcast(BF16)[0:3 * G, 0:N]
                act.activation(partsT[s][:], src, ACT.Copy).then_inc(partsT_ok[s], 1)

            def qkn(at, s, j):
                for a in range(2 * j, 2 * j + 2):
                    act.wait_ge(qk_normed[s], qk_normed.at(at.c, a + 1))
                    v = slot[s][:, a, :]
                    act.activation(v, v, ACT.Exp, scale=1.0 if j == 0 else -1.0).then_inc(qk_exp[s], 1)

            def y(at, s, j):
                act.wait_ge(y_ok[s], y_ok.at(at.c, j + 1))
                act.activation(cTh[s][:, j, :], slot[s][:, 2 + j, :], ACT.Copy).then_inc(c_hi[s], 1)

            def swiglu(at, s, i):
                tiles = HT1 if at.name == "f1" else HT0
                if i < tiles:
                    m = rows_of(at.name, i)
                    act.wait_ge(full[at.bank("g")], at.filled("g"))
                    g = bank[at.bank("g")]
                    if at.name == "f1" and i == 0:
                        act.activation(slot[s][0:M0 + E1, 0, :], g[0:M0 + E1, :], ACT.Copy,
                                       scale=IWS).then_inc(g_in[s], 1)
                    act.wait_ge(h_ok, at.tile(i, 2))
                    r = (at.number(i)) % 2
                    act.activation(sg[0:m, r, :], g[0:m, :], ACT.Silu, scale=IWS).then_inc(silu_ok, 1)
                j = i - 1
                if 0 <= j < tiles:
                    m = rows_of(at.name, j)
                    act.wait_ge(h_ok, at.tile(j))
                    act.wait_ge(down_ok, at.tile(j, HR))
                    n = at.number(j)
                    act.activation(hTh[0:m, n % HR, :], h32[0:m, n % 2, :], ACT.Copy).then_inc(h_hi, 1)

            def route(at, s, m):
                act.wait_ge(soft_in[s], soft_in.at(at.c, m + 1))
                act.activation(prob[s][:], prob[s][:], ACT.Exp).then_inc(soft_exp[s], 1)

            def h112(at, s, i):
                act.wait_ge(full[at.bank()], at.filled())
                act.activation(slot[s][0:HL, 0, :], bank[at.bank()][0:HL, :], ACT.Copy,
                               scale=IWS).then_inc(h_in[s], 1)

            def hw(at, s, i):
                act.wait_ge(hw_ok[s], hw_ok.at(at.c, 1))
                act.activation(hwh[0:HL, :], slot[s][0:HL, 0, :], ACT.Copy).then_inc(hw_hi[s], 1)

            def pjs(at, s, j):
                act.wait_ge(hist_ok[s], at.it + 1)
                act.wait_ge(full[at.bank()], at.filled())
                act.activation(pj[s][:, j, HIST:], bank[at.bank()][:], ACT.Copy, scale=IWS).then_inc(pj_in[s], 1)
                act.wait_ge(pj_in[s], pj_in.at(at.c, j + 1))
                act.activation(slot[s][:, j, :], pj[s][:, j, 0:N], ACT.Identity, bias=smc("conv_b", j, 1),
                               scale=smc("conv_w", j * DCONV, 1)).then_inc(tap0[s], 1)

            def silu(at, s, j):
                act.wait_ge(conv_ok[s], conv_ok.at(at.c, j + 1))
                v = slot[s][:, j, :]
                act.activation(v, v, ACT.Silu).then_inc(X_ok[s], 1)

            def dts(at, s, j):
                act.wait_ge(full[at.bank()], at.filled())
                v = slot[s][:, 4 + j, :]
                act.activation(v, bank[at.bank()][:], ACT.Abs, bias=smc("dt_b", j, 1)).then_inc(dt_abs[s], 1)
                act.wait_ge(dt_abs[s], dt_abs.at(at.c, j + 1))
                act.activation(v, v, ACT.Exp, scale=-1.0).then_inc(dt_exp[s], 1)

            def softplus(at, s, j):
                act.wait_ge(dt_exp[s], dt_exp.at(at.c, j + 1))
                v = slot[s][:, 4 + j, :]
                act.activation(v, v, ACT.Ln, bias=1.0).then_inc(dt_ln[s], 1)

            def ct(at, s, j):
                act.wait_ge(dt_ok[s], dt_ok.at(at.c, j + 1))
                act.activation(pj[s][:, j, HIST:], slot[s][:, 4 + j, :], ACT.Exp,
                               scale=negA[:, j:j + 1]).then_inc(decay_ok[s], 1)
                if j >= 2:
                    act.wait_ge(comb_ok[s], comb_ok.at(at.c, j - 1))
                act.wait_ge(full[at.bank("gate")], at.filled("gate"))
                act.activation(slot[s][:, 8 + j % 2, :], bank[at.bank("gate")][:], ACT.Tanh,
                               scale=0.5 * IWS).then_inc(tanh_ok[s], 1)

            def comb(at, s, j):
                act.wait_ge(comb_ok[s], comb_ok.at(at.c, j + 1))
                act.activation(cTh[s][:, j, :], slot[s][:, j, :], ACT.Copy).then_inc(c_hi[s], 1)

            def prep(at, s, i):
                act.wait_ge(consts_in, 32)
                act.activation(negA[:], smc("A_log"), ACT.Exp).then_inc(prep_a, 1)
                act.wait_ge(consts_ok, 1)

            act.sem_inc(silu_ok, 1)
            act.sem_inc(h_hi, 1)
            walk(act, dict(piece=piece, prep=prep, rms=rms, T=T, qkv=qkv, spread=spread, qkn=qkn, y=y, f0=swiglu, f1=swiglu,
                           route=route, h112=h112, hw=hw, pj=pjs, silu=silu, dt=dts, softplus=softplus, ct=ct, comb=comb))

        @block.vector
        def _(dve):
            def pause(s):
                dve.memset(idle[:, s:s + 1], 0.0)

            def piece(at, s, j):
                a, n = j * PC, min(PC, W_COLS - j * PC)
                dve.wait_ge(piece_in[j % 2], 16 * (j // 2 + 1))
                dve.wait_ge(piece_hi, j + 1)
                stage = pj[j % 2][:].rearrange("p a n -> p (a n)")
                dve.scalar_tensor_tensor(out=Wl[:, a:a + n], in0=stage[:, 0:n], scalar=WS, in1=Wh[:, a:a + n],
                                         op0=ALU.mult, op1=ALU.subtract).then_inc(piece_lo, 1)
                if j == PIECES - 1:
                    dve.wait_ge(piece_lo, PIECES)
                    for s in range(B):
                        dve.memset(pj[s][:, :, 0:HIST], 0.0).then_inc(hist_ok[s], 1)

            def xn(at, s, i):
                own_v.start(s)
                dve.wait_ge(x_in[s], x_in.at(at.c, 16))
                dve.wait_ge(rstd[s], rstd.at(at.c, 1))
                dst = slot[s][:, 0:2, :].rearrange("p a (t d) -> p (a t) d", d=D)
                for t in range(TT):
                    ins = dve.tensor_scalar(dst[:, t, :], xin[s][:, t, :], stat[s][:, 2, t:t + 1], None, ALU.mult)
                ins.then_inc(normed[s], 1)

            def T(at, s, t):
                for k in range(KD):
                    dve.wait_ge(full[at.bank(k)], at.filled(k))
                    src = bank[at.bank(k)]
                    dve.wait_ge(xT_hi[s], xT_hi.at(at.c, 2 * t + k + 1))
                    dve.tensor_tensor(xTl[s][:, k, :], src[:], xTh[s][:, k, :],
                                      ALU.subtract).then_inc(xT_lo[s], 1)

            def sumsq(at, s, i):
                dve.wait_ge(full[at.bank()], at.filled())
                src = bank[at.bank()][:, 0:TT * G].rearrange("p (t g) -> p t g", g=G)
                dve.tensor_scalar(rest[s][:, :, 0:2], src[:, :, 0:2], 1.0 / D, EPS_RMS, ALU.mult,
                                  ALU.add).then_inc(ms_qk[s], 1)

            def spread(at, s, e):
                if e == 0:
                    dve.wait_ge(rqk_ok[s], rqk_ok.at(at.c, 1))
                dve.wait_ge(partsT_ok[s], partsT_ok.at(at.c, e))
                p = parts[s]
                dve.tensor_copy(p[:, :, 0, :], small8[s][:]).then_inc(own_v[s], own_v.one(s))
                dve.wait_ge(own_v[s], own_v.last(s, at.c))
                dve.tensor_tensor(rest[s][:], small8[s][:], p[:, :, 0, :], ALU.subtract).then_inc(own_v[s], own_v.one(s))
                dve.wait_ge(own_v[s], own_v.last(s, at.c))
                dve.tensor_copy(p[:, :, 1, :], rest[s][:]).then_inc(own_v[s], own_v.one(s))
                dve.wait_ge(own_v[s], own_v.last(s, at.c))
                dve.tensor_tensor(p[:, :, 2, :], rest[s][:], p[:, :, 1, :],
                                  ALU.subtract).then_inc(parts_ok[s], 1)

            def qkn(at, s, j):
                dve.wait_ge(full[at.bank()], at.filled())
                src = bank[at.bank()]
                for a in range(2 * j, 2 * j + 2):
                    dve.wait_ge(qkv_in[s], qkv_in.at(at.c, a + 1))
                    v = slot[s][:, a, :]
                    dve.tensor_tensor(v, v, src[:], ALU.mult).then_inc(qk_normed[s], 1)

            def cum(at, s, j):
                dve.wait_ge(qk_exp[s], qk_exp.at(at.c, j + 1))
                dve.wait_ge(qkv_in[s], qkv_in.at(at.c, 5 + j))
                w, q, v = slot[s][:, j, :], slot[s][:, 2 + j, :], slot[s][:, 4 + j, :]
                sum_wv, sum_w = slot[s][:, 6 + j, :], slot[s][:, 8 + j, :]
                dve.tensor_tensor(v, v, w, ALU.mult).then_inc(own_v[s], own_v.one(s))
                dve.wait_ge(own_v[s], own_v.last(s, at.c))
                dve.tensor_tensor_scan(sum_wv, v, zero[:].to_broadcast([P, N]), carry0[s][:, j:j + 1], ALU.add, ALU.add).then_inc(own_v[s], own_v.one(s))
                dve.tensor_tensor_scan(sum_w, w, zero[:].to_broadcast([P, N]), carry0[s][:, 2 + j:3 + j], ALU.add,
                                       ALU.add).then_inc(own_v[s], own_v.one(s))
                dve.wait_ge(own_v[s], own_v.last(s, at.c))
                dve.wait_ge(qk_exp[s], qk_exp.at(at.c, 3 + j))
                dve.scalar_tensor_tensor(out=q, in0=q, scalar=1.0, in1=sum_w, op0=ALU.add, op1=ALU.mult).then_inc(own_v[s], own_v.one(s))
                last = slot[s][:, 6 + j:10:2, N - 1]
                dve.tensor_copy(carry0[s][:, j:j + 3:2], last).then_inc(own_v[s], own_v.one(s))
                dve.wait_ge(own_v[s], own_v.last(s, at.c))
                dve.reciprocal(q, q).then_inc(den_ok[s], 1)

            def ln(at, s, n):
                if n == 0:
                    dve.wait_ge(x2[s], x2.at(at.c, 1))
                if n in (0, 3):
                    tiles = HT0 if n == 0 else HT1
                    dve.wait_ge(down_ok, at.tile(tiles - 1, name="f0" if n == 0 else "f1"))
                out = Place(at.region, at.it, "out", s, n)
                for h in range(2):
                    src = bank[h]
                    if n in (1, 2):
                        dve.wait_ge(full[out.bank(h)], out.filled(h))
                        src = bank[out.bank(h)]
                    z = tok[s][:, 2 * h:2 * h + 2, :]
                    dve.scalar_tensor_tensor(out=z, in0=src[:].rearrange("p (t d) -> p t d", d=D),
                                             scalar=IWS, in1=z, op0=ALU.mult, op1=ALU.add).then_inc(own_v[s], own_v.one(s))
                dve.wait_ge(own_v[s], own_v.last(s, at.c))
                for t in range(TT):
                    ins = dve.bn_stats(bn[s][:, t, :], tok[s][:, t, :])
                ins.then_inc(own_v[s], own_v.one(s))
                dve.wait_ge(own_v[s], own_v.last(s, at.c))
                pause(s)
                for t in range(TT):
                    ins = dve.bn_aggr(mv[s][:, t, :], bn[s][:, t, :])
                ins.then_inc(var[s], 1)

            def norm(at, s, n):
                dve.wait_ge(rstd[s], rstd.at(at.c, n + 2))
                for t in range(TT):
                    v = tok[s][:, t, :]
                    ins = dve.tensor_scalar(v, v, mv[s][:, t, 0:1], stat[s][:, 2, t:t + 1], ALU.subtract, ALU.mult)
                ins.then_inc(normed[s], 1)

            def route(at, s, m):
                e = E0 if m == 0 else E1
                dve.wait_ge(full[at.bank()], at.filled())
                at0 = ER if m == 0 else M0
                src = bank[at.bank()][:].rearrange("p (t g) -> p t g", g=P)[:, :, at0:at0 + e]
                lg = logit[s][:, m, :, :]
                if m == 0:
                    ins = dve.tensor_tensor(lg[:, :, 0:e], src, smc("b_router").unsqueeze(1).to_broadcast([P, TT, E0]),
                                            ALU.add)
                else:
                    ins = dve.tensor_copy(lg[:, :, 0:e], src)
                ins.then_inc(logits[s], 1)
                dve.wait_ge(logits[s], logits.at(at.c, m + 1))
                pause(s)
                for t in range(TT):
                    ins = dve.max(top8[s][:, t, :], lg[:, t, :])
                ins.then_inc(own_v[s], own_v.one(s))
                dve.wait_ge(own_v[s], own_v.last(s, at.c))
                dve.tensor_tensor(prob[s][:], lg, top8[s][:, :, 0:1].to_broadcast([P, TT, G]),
                                  ALU.subtract).then_inc(soft_in[s], 1)
                for t in range(TT):
                    ins = dve.max_index(idx8[s][:, t, :], top8[s][:, t, :], lg[:, t, :])
                ins.then_inc(own_v[s], own_v.one(s))
                dve.wait_ge(own_v[s], own_v.last(s, at.c))
                num = iota[:].unsqueeze(1).to_broadcast([P, TT, G])
                for j in range(2):
                    dve.tensor_tensor(mask[s][:, j, :, :], num,
                                      idx8[s][:, :, j:j + 1].to_broadcast([P, TT, G]), ALU.is_equal).then_inc(own_v[s], own_v.one(s))
                dve.wait_ge(own_v[s], own_v.last(s, at.c))
                dve.tensor_tensor(mask[s][:, 0, :, :], mask[s][:, 0, :, :], mask[s][:, 1, :, :],
                                  ALU.add).then_inc(own_v[s], own_v.one(s))
                dve.wait_ge(own_v[s], own_v.last(s, at.c))

            def soft(at, s, m):
                dve.wait_ge(soft_exp[s], soft_exp.at(at.c, m + 1))
                st = sm_stat[s]
                pr = prob[s][:]
                dve.tensor_reduce(st[:, 0, :], pr, AX_X, ALU.add).then_inc(own_v[s], own_v.one(s))
                dve.wait_ge(own_v[s], own_v.last(s, at.c))
                dve.reciprocal(st[:, 1, :], st[:, 0, :]).then_inc(own_v[s], own_v.one(s))
                dve.wait_ge(own_v[s], own_v.last(s, at.c))
                dve.tensor_tensor(pr, pr, st[:, 1, :].unsqueeze(2).to_broadcast([P, TT, G]),
                                  ALU.mult).then_inc(own_v[s], own_v.one(s))
                dve.wait_ge(own_v[s], own_v.last(s, at.c))
                if m == 0:
                    dve.tensor_tensor(small8[s][:], pr, mask[s][:, 0, :, :], ALU.mult).then_inc(own_v[s], own_v.one(s))
                    dve.wait_ge(own_v[s], own_v.last(s, at.c))
                    dve.memset(small8[s][:, :, E0:E0 + 1], 1.0).then_inc(own_v[s], own_v.one(s))
                    dve.wait_ge(own_v[s], own_v.last(s, at.c))
                    return
                dve.tensor_tensor(pr, pr, mask[s][:, 0, :, :], ALU.mult).then_inc(own_v[s], own_v.one(s))
                dve.wait_ge(own_v[s], own_v.last(s, at.c))
                dve.tensor_reduce(st[:, 2, :], pr, AX_X, ALU.add).then_inc(own_v[s], own_v.one(s))
                dve.wait_ge(own_v[s], own_v.last(s, at.c))
                dve.tensor_scalar(st[:, 2, :], st[:, 2, :], 1e-20, None, ALU.add).then_inc(own_v[s], own_v.one(s))
                dve.wait_ge(own_v[s], own_v.last(s, at.c))
                dve.reciprocal(st[:, 1, :], st[:, 2, :]).then_inc(own_v[s], own_v.one(s))
                dve.wait_ge(own_v[s], own_v.last(s, at.c))
                dve.tensor_tensor(small8[s][:], pr,
                                  st[:, 1, :].unsqueeze(2).to_broadcast([P, TT, G]), ALU.mult).then_inc(own_v[s], own_v.one(s))
                dve.wait_ge(own_v[s], own_v.last(s, at.c))

            def hw(at, s, i):
                dve.wait_ge(full[at.bank()], at.filled())
                src = bank[at.bank()]
                dve.wait_ge(h_in[s], h_in.at(at.c, 1))
                v = slot[s][0:HL, 0, :]
                dve.tensor_tensor(v, v, src[0:HL, :], ALU.mult).then_inc(hw_ok[s], 1)

            def pjs(at, s, j):
                dve.wait_ge(tap0[s], tap0.at(at.c, j + 1))
                v = slot[s][:, j, :]
                for k in range(1, DCONV):
                    ins = dve.scalar_tensor_tensor(out=v, in0=pj[s][:, j, k:k + N],
                                                   scalar=smc("conv_w", j * DCONV + k, 1), in1=v, op0=ALU.mult,
                                                   op1=ALU.add)
                    if k < DCONV - 1:
                        ins.then_inc(own_v[s], own_v.one(s))
                        dve.wait_ge(own_v[s], own_v.last(s, at.c))
                ins.then_inc(conv_ok[s], 1)
                if j == CT - 1:
                    dve.tensor_copy(pj[s][:, :, 0:HIST], pj[s][:, :, N:N + HIST]).then_inc(hist_ok[s], 1)

            def dts(at, s, j):
                dve.wait_ge(full[at.bank()], at.filled())
                dve.wait_ge(dt_abs[s], dt_abs.at(at.c, j + 1))
                dve.wait_ge(hist_ok[s], at.it + 2)
                dve.tensor_scalar(pj[s][:, j, HIST:], bank[at.bank()][:], smc("dt_b", j, 1), 0.0, ALU.add,
                                  ALU.max).then_inc(dt_pos[s], 1)

            def ct(at, s, j):
                X, drive = slot[s][:, j, :], slot[s][:, 4 + j, :]
                dve.wait_ge(decay_ok[s], decay_ok.at(at.c, j + 1))
                dve.scalar_tensor_tensor(out=drive, in0=drive, scalar=BC[:, j:j + 1], in1=X, op0=ALU.mult,
                                         op1=ALU.mult).then_inc(drive_ok[s], 1)
                dve.wait_ge(drive_ok[s], drive_ok.at(at.c, j + 1))
                dve.tensor_tensor_scan(drive, pj[s][:, j, HIST:], drive,
                                       carry1[s][:, j:j + 1], ALU.mult, ALU.add).then_inc(own_v[s], own_v.one(s))
                dve.wait_ge(own_v[s], own_v.last(s, at.c))
                dve.tensor_copy(carry1[s][:, j:j + 1], drive[:, N - 1:N])
                dve.scalar_tensor_tensor(out=X, in0=X, scalar=Dh[:, j:j + 1], in1=drive,
                                         op0=ALU.mult, op1=ALU.add).then_inc(own_v[s], own_v.one(s))
                dve.wait_ge(own_v[s], own_v.last(s, at.c))
                dve.wait_ge(tanh_ok[s], tanh_ok.at(at.c, j + 1))
                dve.scalar_tensor_tensor(out=X, in0=slot[s][:, 8 + j % 2, :], scalar=1.0, in1=X, op0=ALU.add,
                                         op1=ALU.mult).then_inc(comb_ok[s], 1)

            def swiglu(at, s, i):
                one = at.name == "f1"
                if i >= (HT1 if one else HT0):
                    return
                m = rows_of(at.name, i)
                dve.wait_ge(silu_ok, at.tile(i))
                dve.wait_ge(h_hi, at.tile(i, 2))
                dve.wait_ge(h_lo, at.tile(i, 2))
                r = (at.number(i)) % 2
                h = h32[0:m, r, :]
                dve.wait_ge(full[at.bank("u")], at.filled("u"))
                ins = dve.scalar_tensor_tensor(out=h, in0=bank[at.bank("u")][0:m, :], scalar=IWS, in1=sg[0:m, r, :],
                                               op0=ALU.mult, op1=ALU.mult)
                if one and i >= SH:
                    ins.then_inc(own_v[s], own_v.one(s))
                    dve.wait_ge(own_v[s], own_v.last(s, at.c))
                    dve.wait_ge(full[at.bank("cw")], at.filled("cw"))
                    ins = dve.tensor_tensor(h, h, bank[at.bank("cw")][0:m, :], ALU.mult)
                ins.then_inc(h_ok, 1)

            def prep(at, s, i):
                dve.wait_ge(consts_in, 32)
                stage = slot[1][:, 0:5, :].rearrange("p a n -> p (a n)")
                dve.tensor_copy(ident[:], stage[:, 0:P]).then_inc(ident_ok, 1)
                dve.tensor_copy(identb[:], stage[:, 0:P])
                dve.tensor_copy(iota[:], stage[:, P:P + G])
                dve.tensor_copy(sel[:], stage[:, P + G:C_COLS]).then_inc(consts_ok, 1)
                dve.scalar_tensor_tensor(out=BC[:], in0=smc("Bp"), scalar=0.5, in1=smc("Cp"), op0=ALU.mult, op1=ALU.mult)
                dve.tensor_scalar(Dh[:], smc("Dp"), 0.5, None, ALU.mult)
                dve.wait_ge(prep_a, 1)
                dve.tensor_scalar(negA[:], negA[:], -1.0, None, ALU.mult).then_inc(prep_v, 1)

            dve.sem_inc(h_ok, 1)
            dve.memset(ones[:], 1.0)
            dve.memset(eps[:, 0, :], EPS_RMS)
            dve.memset(eps[:, 1, :], EPS_LN)
            dve.memset(neghalf[:], -0.5).then_inc(filled_ok, 1)
            dve.memset(hwh[:], 1.0)
            dve.memset(hwl[:], 0.0)
            dve.memset(zero[:], 0.0)
            for s in range(B):
                dve.memset(small8[s][:], 0.0)
                dve.memset(logit[s][:], NEG)
                dve.memset(carry0[s][:, 0:KD], 0.0)
                dve.memset(carry0[s][:, KD:], 1e-06)
                dve.memset(carry1[s][:], 0.0)
            walk(dve, dict(piece=piece, prep=prep, xn=xn, T=T, sumsq=sumsq, spread=spread, qkn=qkn, cum=cum, ln=ln, norm=norm,
                           route=route, soft=soft, hw=hw, pj=pjs, dt=dts, ct=ct, f0=swiglu, f1=swiglu))

        @block.gpsimd
        def _(pool):
            def pause(s):
                pool.tensor_tensor(idle[:, B + s:B + s + 1], ones[:], ones[:], ALU.mult)

            def rms(at, s, i):
                own_p.start(s)
                pool.wait_ge(normed[s], normed.at(at.c, 0))
                pool.wait_ge(squares[s], squares.at(at.c, 1))
                st = stat[s]
                pool.tensor_tensor(st[:, 1, :], st[:, 0, :], eps[:, 0, :], ALU.add).then_inc(own_p[s], own_p.one(s))
                pool.wait_ge(own_p[s], own_p.last(s, at.c))
                pool.tensor_tensor(st[:, 2, :], st[:, 1, :], neghalf[:, 0:TT], ALU.pow).then_inc(rstd[s], 1)

            def double(at, s, i):
                pool.wait_ge(stored[s], stored.at(at.c, 0))
                pool.wait_ge(x_in[s], x_in.at(at.c, 16))
                pause(s)
                pool.tensor_scalar(tok[s][:], xin[s], 2.0, 1.0, ALU.mult, ALU.mult).then_inc(x2[s], 1)

            def sumsq(at, s, i):
                for j in range(2):
                    pool.wait_ge(sq_in[s], sq_in.at(at.c, 2 * j + 2))
                    a, b = slot[s][:, 6 + 2 * j, :], slot[s][:, 7 + 2 * j, :]
                    pool.tensor_tensor(a, a, b, ALU.add).then_inc(sumsq_in[s], 1)

            def rqk(at, s, i):
                pool.wait_ge(ms_qk[s], ms_qk.at(at.c, 1))
                half = neghalf[:].rearrange("p (t g) -> p t g", g=G)[:, :, 0:2]
                pool.tensor_tensor(small8[s][:, :, 0:2], rest[s][:, :, 0:2], half, ALU.pow).then_inc(rqk_ok[s], 1)

            def y(at, s, j):
                pool.wait_ge(den_ok[s], den_ok.at(at.c, j + 1))
                v = slot[s][:, 2 + j, :]
                pool.tensor_tensor(v, v, slot[s][:, 6 + j, :], ALU.mult).then_inc(y_ok[s], 1)
                pool.wait_ge(c_hi[s], c_hi.at(at.c, j + 1))
                pool.tensor_tensor(cTl[s][:, j, :], v, cTh[s][:, j, :], ALU.subtract).then_inc(c_lo[s], 1)

            def ln(at, s, n):
                pool.wait_ge(var[s], var.at(at.c, n + 1))
                st = stat[s]
                pool.tensor_tensor(st[:, 1, :], mv[s][:, :, 1], eps[:, 1, :], ALU.add).then_inc(own_p[s], own_p.one(s))
                pool.wait_ge(own_p[s], own_p.last(s, at.c))
                pool.tensor_tensor(st[:, 2, :], st[:, 1, :], neghalf[:, 0:TT], ALU.pow).then_inc(rstd[s], 1)

            def hw(at, s, i):
                pool.wait_ge(hw_hi[s], hw_hi.at(at.c, 1))
                pool.tensor_tensor(hwl[0:HL, :], slot[s][0:HL, 0, :], hwh[0:HL, :],
                                   ALU.subtract).then_inc(hw_lo[s], 1)

            def softplus(at, s, j):
                pool.wait_ge(dt_ln[s], dt_ln.at(at.c, j + 1))
                pool.wait_ge(dt_pos[s], dt_pos.at(at.c, j + 1))
                v = slot[s][:, 4 + j, :]
                pool.tensor_tensor(v, v, pj[s][:, j, HIST:], ALU.add).then_inc(dt_ok[s], 1)

            def comb(at, s, j):
                pool.wait_ge(c_hi[s], c_hi.at(at.c, 3 + j))
                pool.tensor_tensor(cTl[s][:, j, :], slot[s][:, j, :], cTh[s][:, j, :],
                                   ALU.subtract).then_inc(c_lo[s], 1)

            def swiglu(at, s, i):
                j = i - 1
                if not 0 <= j < (HT1 if at.name == "f1" else HT0):
                    return
                m = rows_of(at.name, j)
                pool.wait_ge(h_hi, at.tile(j))
                n = at.number(j)
                pool.tensor_tensor(hTl[0:m, n % HR, :], h32[0:m, n % 2, :], hTh[0:m, n % HR, :],
                                   ALU.subtract).then_inc(h_lo, 1)

            pool.sem_inc(h_lo, 1)
            pool.wait_ge(filled_ok, 1)
            walk(pool, dict(rms=rms, double=double, sumsq=sumsq, rqk=rqk, y=y, ln=ln, hw=hw, softplus=softplus, comb=comb,
                            f0=swiglu, f1=swiglu))


def _rows(w):
    k, m = w.shape
    t = -(-k // P)
    full = np.zeros((t * P, m), w.dtype)
    full[:k] = w
    return full.reshape(t, P, m).transpose(1, 0, 2).reshape(P, t * m)


def _laid_out(i):
    qkv = i["L0_attn_w_qkv"].T
    down = i["L1_ffn_sw_down"].T
    parts = {
        "qkv": _rows(np.concatenate([qkv[:, D:2 * D], qkv[:, :D], qkv[:, 2 * D:]], 1)),
        "swi": _rows(i["L0_attn_w_swiglu"].T),
        "wo": _rows(i["L0_attn_w_out"].T),
        "lora_a": _rows(np.concatenate([i["L0_ffn_A_r"].transpose(1, 0, 2).reshape(D, ER), i["L0_ffn_W_router"],
                                        i["L0_ffn_A_s"]], 1)),
        "base": _rows(i["L0_ffn_W_base"]),
        "lora_b": _rows(np.concatenate([i["L0_ffn_B_r"].reshape(ER, D), np.zeros((E0, D), np.float32), i["L0_ffn_B_s"],
                                        i["L0_ffn_b_base"][None]], 0)),
        "inp": _rows(i["L1_attn_in_proj_w"].T),
        "gatep": _rows(i["L1_attn_gate_proj_w"].T),
        "outp": _rows(i["L1_attn_out_proj_w"].T),
        "eg": _rows(np.concatenate([i["L1_ffn_sw_gate"][:M0], i["L1_ffn_gate_weight"], i["L1_ffn_sw_gate"][M0:],
                                    i["L1_ffn_w_gate"].reshape(-1, D)], 0).T),
        "eu": _rows(np.concatenate([i["L1_ffn_sw_up"], i["L1_ffn_w_up"].reshape(-1, D)], 0).T),
        "ed": _rows(np.concatenate([down[:M0], np.zeros((P - M0, D), np.float32), down[M0:],
                                    i["L1_ffn_w_down"].transpose(0, 2, 1).reshape(-1, D)], 0)),
    }
    wpack = np.concatenate([parts[n] for n, _ in W_PARTS], 1)

    def per_channel(v):
        return v.reshape(CT, P, -1).transpose(1, 0, 2).reshape(P, -1)

    hd = INNER // NH
    dt_w = np.zeros((CT, P, P), np.float32)
    for h in range(NH):
        c = h * hd
        rows = slice(c % P, c % P + hd)
        dt_w[c // P, rows, rows] = i["L1_attn_dt_w"][h][:, None]
    sparts = {
        "conv_w": per_channel(i["L1_attn_conv_w"]), "conv_b": per_channel(i["L1_attn_conv_b"]),
        "A_log": per_channel(i["L1_attn_A_log"]), "Bp": per_channel(i["L1_attn_Bp"]),
        "Cp": per_channel(i["L1_attn_Cp"]), "Dp": per_channel(i["L1_attn_Dp"]),
        "dt_b": per_channel(np.repeat(i["L1_attn_dt_b"], hd)),
        "dt_w": dt_w.transpose(1, 0, 2).reshape(P, CT * P),
        "b_router": np.broadcast_to(i["L0_ffn_b_router"], (P, E0)),
    }
    small = np.concatenate([sparts[n] for n, _ in S_PARTS], 1)
    return {"in_x_dram": i["L0_attn_x"], "in_wpack_dram": wpack, "in_small_dram": small,
            "in_const_dram": constants()}


def kernel(**inputs):
    import concourse.bacc as _bacc
    from concourse.bass_utils import run_bass_kernel_spmd as _run

    nc = _bacc.Bacc("TRN2", target_bir_lowering=False, num_devices=1)
    arrays = _laid_out({n: np.ascontiguousarray(a) for n, a in inputs.items()})
    arrays = {n: np.ascontiguousarray(a) for n, a in arrays.items()}
    args = [nc.dram_tensor(n, a.shape, mybir.dt.from_np(a.dtype), kind="ExternalInput").ap()
            for n, a in arrays.items()]
    args.append(nc.dram_tensor("out_0_dram", (B, S, D), F32, kind="ExternalOutput").ap())
    nc.disable_value_cache = True
    bass_two_postnorm_layers(nc, *args)
    r = _run(nc, [arrays], core_ids=[0])
    return r.results[0]["out_0_dram"]
```
